# Optimizing a Trainium2 kernel written in Bass

```python
import numpy as np
import jax
import jax.numpy as jnp

def _softmax(x, axis=-1):
    return jax.nn.softmax(x, axis=axis)

def _gelu(x):
    return jax.nn.gelu(x, approximate=True)

def _silu(x):
    return jax.nn.silu(x)

def _sigmoid(x):
    return jax.nn.sigmoid(x)

def _layernorm(x, axis=-1, eps=1e-05):
    m = jnp.mean(x, axis=axis, keepdims=True)
    v = jnp.var(x, axis=axis, keepdims=True)
    return (x - m) / jnp.sqrt(v + eps)

def _scatter_add(tgt, idx, src, axis=0):
    return tgt.at[idx].add(src)

def _segment_sum(src, seg, n):
    return jax.ops.segment_sum(src, seg, n)
kernel_name = 'mk_flamingo_gated_d1_seqx_r4_828ff6'

def setup_inputs(seed: int=0):
    np.random.seed(seed)
    _w = jnp.asarray

    def _rec_inputs():
        import jax
        import jax.numpy as jnp
        _rk = jax.random.key(seed)
        x = -0.000125 + 0.9999 * jax.random.normal(jax.random.fold_in(_rk, 1), (8, 256, 1024), jnp.float32)
        _lenS = 256 - jax.random.randint(jax.random.fold_in(_rk, 7), (8,), 0, max(1, 256 // 4) + 1, jnp.int32)
        _lenS2 = 256 - jax.random.randint(jax.random.fold_in(_rk, 8), (8,), 0, max(1, 256 // 4) + 1, jnp.int32)
        _ctx_4096P = jax.random.normal(jax.random.fold_in(_rk, 11), (8, 16, 1024), jnp.float32)
        _ctx_4096c = jax.random.dirichlet(jax.random.fold_in(_rk, 511), 0.3 * jnp.ones((16,), jnp.float32), (8, 256))
        _ctx_4096t = jnp.einsum('bsk,bkd->bsd', _ctx_4096c, _ctx_4096P)
        _ctx_4096t = _ctx_4096t * jax.lax.rsqrt(jnp.mean(jnp.square(_ctx_4096t)) + 1e-12) * 0.953939
        ctx_4096 = -1.52775e-05 + 0.999936 * (_ctx_4096t + 0.3 * jax.random.normal(jax.random.fold_in(_rk, 611), (8, 256, 1024), jnp.float32))
        _g = jax.random.normal(jax.random.fold_in(_rk, 9001), (2, 1), jnp.float32)
        _g = jnp.sign(_g) * jnp.maximum(jnp.abs(_g), 1.0) + (_g == 0) * 1.0
        g_xattn = _g[0]
        g_ffn = _g[1]
        return (x, ctx_4096, g_xattn, g_ffn)
    x, ctx_4096, g_xattn, g_ffn = _rec_inputs()

    def _L0_xattn_setup():
        import jax, jax.numpy as jnp
        import numpy as np
        H = 8
        C = 2

        def _autocorrelation(Q, K, V):
            B, L, D = Q.shape
            d = D // H
            q = Q.reshape(B, L, H, d).transpose(0, 2, 1, 3)
            k = K.reshape(B, L, H, d).transpose(0, 2, 1, 3)
            v = V.reshape(B, L, H, d).transpose(0, 2, 1, 3)
            qf = jnp.fft.fft(q, axis=2)
            kf = jnp.fft.fft(k, axis=2)
            corr = jnp.fft.ifft(qf * jnp.conj(kf), axis=2).real
            topk = int(C * np.log(L))
            w, idx = jax.lax.top_k(corr.transpose(0, 1, 3, 2), topk)
            w = jax.nn.softmax(w, axis=-1)
            pos = jnp.arange(L)[:, None]
            out = jnp.zeros_like(v)
            for i in range(topk):
                g = jnp.minimum(idx[:, :, None, :, i] + pos, L - 1)
                out = out + w[:, :, None, :, i] * jnp.take_along_axis(v, g, axis=2)
            return out.transpose(0, 2, 1, 3).reshape(B, L, D)
        key = jax.random.key(seed)
        k1, k2, k3 = jax.random.split(key, 3)
        B, L, D = (16, 128, 1024)
        Q = jax.random.normal(k1, (B, L, D), dtype=jnp.float32)
        K = jax.random.normal(k2, (B, L, D), dtype=jnp.float32)
        V = jax.random.normal(k3, (B, L, D), dtype=jnp.float32)
        return {'Q': Q, 'K': K, 'V': V}
    _L0_xattn_all = _L0_xattn_setup()
    _L0_xattn_in = {k: v for k, v in _L0_xattn_all.items() if k in ()}
    del _L0_xattn_all

    def _L0_ffn_setup():
        import jax, jax.numpy as jnp
        import numpy as np
        B_SZ, S, D_IN, D_OUT = (4, 1024, 1024, 1024)
        E, R = (16, 16)
        key = jax.random.key(seed)
        ks = jax.random.split(key, 6)
        x = jax.random.normal(ks[0], (B_SZ, S, D_IN), dtype=jnp.float32)
        W = jax.random.normal(ks[1], (D_OUT, D_IN), dtype=jnp.float32) * (1.0 / np.sqrt(D_IN))
        b = jax.random.normal(ks[2], (D_OUT,), dtype=jnp.float32) * 0.01
        A = jax.random.normal(ks[3], (E, R, D_IN), dtype=jnp.float32) * (1.0 / np.sqrt(D_IN))
        Bw = jax.random.normal(ks[4], (E, D_OUT, R), dtype=jnp.float32) * (1.0 / np.sqrt(R))
        probs = jax.random.uniform(ks[5], (E,), dtype=jnp.float32)
        probs = probs / jnp.sum(probs)
        return {'x': x, 'W': W, 'b': b, 'A': A, 'B': Bw, 'probs': probs}
    _L0_ffn_all = _L0_ffn_setup()
    _L0_ffn_in = {k: v for k, v in _L0_ffn_all.items() if k in ('W', 'b', 'A', 'B', 'probs')}
    del _L0_ffn_all
    return {'x': x, 'ctx_4096': ctx_4096, 'g_xattn': g_xattn, 'g_ffn': g_ffn, 'L0_ffn_W': _L0_ffn_in['W'], 'L0_ffn_b': _L0_ffn_in['b'], 'L0_ffn_A': _L0_ffn_in['A'], 'L0_ffn_B': _L0_ffn_in['B'], 'L0_ffn_probs': _L0_ffn_in['probs']}

def reference(x, ctx_4096, g_xattn, g_ffn, L0_ffn_W, L0_ffn_b, L0_ffn_A, L0_ffn_B, L0_ffn_probs):
    import jax
    import jax.numpy as jnp

    def _L0_xattn_ref(Q, K, V):
        import jax, jax.numpy as jnp
        import numpy as np
        H = 8
        C = 2

        def _autocorrelation(Q, K, V):
            B, L, D = Q.shape
            d = D // H
            q = Q.reshape(B, L, H, d).transpose(0, 2, 1, 3)
            k = K.reshape(B, L, H, d).transpose(0, 2, 1, 3)
            v = V.reshape(B, L, H, d).transpose(0, 2, 1, 3)
            qf = jnp.fft.fft(q, axis=2)
            kf = jnp.fft.fft(k, axis=2)
            corr = jnp.fft.ifft(qf * jnp.conj(kf), axis=2).real
            topk = int(C * np.log(L))
            w, idx = jax.lax.top_k(corr.transpose(0, 1, 3, 2), topk)
            w = jax.nn.softmax(w, axis=-1)
            pos = jnp.arange(L)[:, None]
            out = jnp.zeros_like(v)
            for i in range(topk):
                g = jnp.minimum(idx[:, :, None, :, i] + pos, L - 1)
                out = out + w[:, :, None, :, i] * jnp.take_along_axis(v, g, axis=2)
            return out.transpose(0, 2, 1, 3).reshape(B, L, D)
        return _autocorrelation(Q, K, V)

    def _L0_ffn_ref(x, W, b, A, B, probs):
        import jax, jax.numpy as jnp
        import numpy as np
        B_SZ, S, D_IN, D_OUT = (4, 1024, 1024, 1024)
        E, R = (16, 16)
        out = jnp.einsum('bsd,od->bso', x, W) + b
        h = jnp.einsum('bsd,erd->bser', x, A)
        contrib = jnp.einsum('bser,e,eor->bso', h, probs, B)
        return out + contrib
    x = x + jnp.tanh(g_xattn[0]) * _L0_xattn_ref(_layernorm(x, axis=-1), ctx_4096, ctx_4096)
    x = x + jnp.tanh(g_ffn[0]) * _L0_ffn_ref(_layernorm(x, axis=-1), L0_ffn_W, L0_ffn_b, L0_ffn_A, L0_ffn_B, L0_ffn_probs)
    return x

_drawn_inputs = setup_inputs


def setup_inputs(seed=0):
    import zlib

    import numpy as np

    out = dict(_drawn_inputs(seed))
    spreads = {}
    factors = {'L0_ffn_b': 8.0}
    for name, (base, spread) in spreads.items():
        noise = np.random.default_rng([zlib.crc32(name.encode()), seed]).standard_normal(out[name].shape)
        drawn = base * np.exp(spread * noise) if base else spread * noise
        out[name] = jnp.asarray(drawn.astype(out[name].dtype))
    for name, factor in factors.items():
        out[name] = (out[name] * factor).astype(out[name].dtype)
    return out
```

```python
from contextlib import ExitStack

import concourse.bass as bass
from concourse import mybir

F32 = mybir.dt.float32
F32R = mybir.dt.float32r
ALU = mybir.AluOpType
ACT = mybir.ActivationFunctionType

P = 128
BATCH, L, D = 8, 256, 1024
HALF = D // 2
UNITS = 2 * BATCH
TILES = HALF // P
KD = D // P
E, R = 16, 16
TOPK = 11
GONE = -3.0e38
EPS = 1e-5

FC, FS, NC, NS = 0, P, 2 * P, 3 * P
CORR_C, CORR_S = 4 * P, 4 * P + L
OUT = 4 * P + 2 * L
IDENT = OUT + 4 * L
MASK, NSIN = IDENT + P, IDENT + P + 1
TABLE = NSIN + 1

T_FILLS = 6
XW_FILLS = 6
P1_STEPS = 6
P2_STEPS = 12
TOP_STEPS = 24
FOLD_STEPS = 4
LN_STEPS = 6
RS_STEPS = 4
FIX_STEPS = 4
RING = 4


def live(v, n):
    return not isinstance(v, int) or 0 <= v < n


def some(v):
    return not isinstance(v, int) or v > 0


def most(v, n):
    return min(v, n) if isinstance(v, int) else v


def apart(eng, turns):
    eng.sem_inc(turns, 1)


def build(nc, x, ctx_kv, v_last, g_attn, g_ffn, W, bias, A, B, probs, table, out):
    with ExitStack() as ctx:
        def sb(name, shape, dt=F32):
            return ctx.enter_context(nc.sbuf_tensor(name, shape, dt))

        def sem(name):
            return ctx.enter_context(nc.semaphore(name))

        tab = sb("tab", [P, TABLE])
        w_hi = sb("w_hi", [P, KD, D], F32R)
        w_lo = sb("w_lo", [P, KD, D], F32R)
        xr = sb("xr", [P, RING, 2, D])
        qh = sb("qh", [P, 2, HALF])
        vt = sb("vt", [P, 2, D])
        vl = sb("vl", [P, D])
        eq, oq, ev, ov = (sb(n, [P, HALF]) for n in ("eq", "oq", "ev", "ov"))
        Qc, Qs, corr_im, prod = (sb(n, [P, HALF]) for n in ("Qc", "Qs", "corr_im", "prod"))
        V = sb("V", [P, 2, 4, HALF])
        Wsp = sb("Wsp", [P, 4, HALF])
        cyc_im, neg_im = sb("cyc_im", [P, HALF]), sb("neg_im", [P, HALF])
        wfold = sb("wfold", [P, 2, HALF])
        corr = sb("corr", [P, TILES, L])
        left = sb("left", [P, TILES, L])
        prob = sb("prob", [P, TILES, L])
        top = sb("top", [P, TILES, 16])
        top_rel = sb("top_rel", [P, TILES, TOPK])
        top_exp = sb("top_exp", [P, TILES, TOPK])
        top_sum, log_sum, exp_bias = (sb(n, [P, TILES]) for n in ("top_sum", "log_sum", "exp_bias"))
        xhat = sb("xhat", [P, D])
        xT_hi = sb("xT_hi", [P, KD, P], F32R)
        xT_lo = sb("xT_lo", [P, KD, P], F32R)
        gbias = sb("gbias", [P, D])
        stage = sb("stage", [P, 2, D])
        stats = [sb(f"stats{n}", [P, 2, 2, 6]) for n in (1, 2)]
        mv = [sb(f"mv{n}", [P, 2, 2]) for n in (1, 2)]
        var_eps = [sb(f"var_eps{n}", [P, 2]) for n in (1, 2)]
        rstd = [sb(f"rstd{n}", [P, 2]) for n in (1, 2)]
        shift = [sb(f"shift{n}", [P, 2]) for n in (1, 2)]
        consts = sb("consts", [P, 5, 2])
        g_in, g_t = sb("g_in", [P, 2]), sb("g_t", [P, 2])
        pr = sb("pr", [P, 2])

        bank = [ctx.enter_context(nc.psum_tensor(f"bank{n}", [P, 512], F32)) for n in range(8)]
        t_ps, xw_ps, c_ps, fo_ps = bank[0:2], bank[2:4], bank[4:6], bank[6:8]

        pB = xr[:, 2, :, :]
        A_sb = [xhat, gbias]
        W_rows = [stage[:, 0, :], stage[:, 1, :], xr[:, 3, 0, :], xr[:, 3, 1, :]]

        ident = tab[:, IDENT:IDENT + P]
        mask = tab[:, MASK:MASK + 1]

        ld_tab, ld_x, ld_v, ld_vl, ld_g = (sem(n) for n in ("ld_tab", "ld_x", "ld_v", "ld_vl", "ld_g"))
        ld_B, ld_A, ld_W, ld_probs, ld_bias = (sem(n) for n in ("ld_B", "ld_A", "ld_W", "ld_probs", "ld_bias"))
        st_out = [sem("st_lo"), sem("st_hi")]
        g_ready, gbias_ready, basis_ready, consts_ready = (sem(n) for n in ("g_ready", "gbias_ready", "basis_ready",
                                                                           "consts_ready"))
        pB_done, prep_full, prep_hi, prep_lo = (sem(n) for n in ("pB_done", "prep_full", "prep_hi", "prep_lo"))
        xw_full, xw_evac, t_full, t_evac = (sem(n) for n in ("xw_full", "xw_evac", "t_full", "t_evac"))
        ft_full, ft_hi, ft_lo, f_full, f_evac = (sem(n) for n in ("ft_full", "ft_hi", "ft_lo", "f_full", "f_evac"))
        o_full, x1_step, c_full, c_evac = (sem(n) for n in ("o_full", "x1_step", "c_full", "c_evac"))
        top_step, top_act, exp_done = (sem(n) for n in ("top_step", "top_act", "exp_done"))
        p1_step, p2_step, nyq1, nyq2, fix_step = (sem(n) for n in ("p1_step", "p2_step", "nyq1", "nyq2", "fix_step"))
        ln_step = [sem("ln1_step"), sem("ln2_step")]
        rs_step = [sem("rs1_step"), sem("rs2_step")]
        qhat_done, fold_step, xhat_done, gb_added = (sem(n) for n in ("qhat_done", "fold_step", "xhat_done",
                                                                     "gb_added"))
        dve_turns, sp_turns = sem("dve_turns"), sem("sp_turns")
        block = ctx.enter_context(nc.Block())

        def x_tile(b, r):
            return xr[:, b & (RING - 1), r, :]

        def x_half(b, r, h):
            return xr[:, b & (RING - 1), r, h * HALF:(h + 1) * HALF]

        def all_slots(eng, slot):
            for i in (-1, 0, 1):
                slot(i, 0)
                slot(i, 1)
            with eng.Fori(2, 7) as i:
                slot(i, 0)
                slot(i, 1)
            for i in (7, 8, 9):
                slot(i, 0)
                slot(i, 1)

        @block.sync
        def _(sp):
            sp.dma_start(xr[:, 0, :, :], x[0]).then_inc(ld_x, 16)
            sp.dma_start(tab[:, :], table).then_inc(ld_tab, 16)
            sp.dma_start(vt[:, :, :], ctx_kv[0]).then_inc(ld_v, 16)
            sp.dma_start(g_in[:, 0:1], g_attn.partition_broadcast(P)).then_inc(ld_g, 16)
            sp.dma_start(g_in[:, 1:2], g_ffn.partition_broadcast(P)).then_inc(ld_g, 16)
            sp.dma_start(vl[:, :], v_last[0].partition_broadcast(P)).then_inc(ld_vl, 16)
            for q in range(2):
                sp.dma_start(pr[:, q:q + 1],
                             probs[q * 8:(q + 1) * 8].unsqueeze(1).broadcast_to((8, R)).unsqueeze(2)
                             ).then_inc(ld_probs, 16)
            sp.dma_start(pB, B.rearrange("(a p) o -> p a o", p=P)).then_inc(ld_B, 16)
            for q in range(2):
                sp.dma_start(A_sb[q][:, :], A.rearrange("e r d -> (e r) d")[q * P:(q + 1) * P]).then_inc(ld_A, 16)
            for q in range(4):
                sp.dma_start(W_rows[q], W[q * P:(q + 1) * P]).then_inc(ld_W, 16)
            sp.wait_ge(ld_x, 16)
            sp.dma_start(xr[:, 1, :, :], x[1]).then_inc(ld_x, 16)
            sp.wait_ge(fold_step, 2 * FOLD_STEPS)
            sp.dma_start(vt[:, :, :], ctx_kv[1]).then_inc(ld_v, 16)
            sp.wait_ge(prep_full, KD)
            for q in range(4):
                sp.dma_start(W_rows[q], W[(4 + q) * P:(5 + q) * P]).then_inc(ld_W, 16)

            def body(i):
                if live(i - 2, BATCH):
                    sp.wait_ge(f_evac, 4 * (i - 2) + 4)
                    sp.dma_start(out[i - 2, 1], x_tile(i - 2, 1)).then_inc(st_out[1], 16)
                if live(i + 1, BATCH):
                    sp.wait_ge(fix_step, FIX_STEPS * (2 * i + 2))
                    sp.wait_ge(ld_vl, 16 * (i + 1))
                    sp.dma_start(vl[:, :], v_last[i + 1].partition_broadcast(P)).then_inc(ld_vl, 16)
                if live(i - 1, BATCH):
                    sp.wait_ge(f_evac, 4 * (i - 1) + 2)
                    sp.dma_start(out[i - 1, 0], x_tile(i - 1, 0)).then_inc(st_out[0], 16)
                if live(i + 2, BATCH):
                    sp.wait_ge(fold_step, FOLD_STEPS * (2 * i + 4))
                    sp.wait_ge(ld_v, 16 * (i + 2))
                    sp.dma_start(vt[:, :, :], ctx_kv[i + 2]).then_inc(ld_v, 16)
                    if not isinstance(i, int) or i >= 2:
                        for r in range(2):
                            sp.wait_ge(st_out[r], 16 * (i - 1))
                    else:
                        sp.wait_ge(prep_full, 2 * KD)
                    sp.wait_ge(ld_x, 16 * (i + 2))
                    apart(sp, sp_turns)
                    sp.dma_start(xr[:, (i + 2) & (RING - 1), :, :], x[i + 2]).then_inc(ld_x, 16)

            body(0)
            sp.dma_start(gbias[:, :], bias.partition_broadcast(P)).then_inc(ld_bias, 16)
            body(1)
            with sp.Fori(2, 6) as i:
                body(i)
            for i in (6, 7, 8, 9):
                body(i)
            for r in range(2):
                sp.wait_ge(st_out[r], 16 * BATCH)

        @block.tensor
        def _(pe):
            mm = nc.tensor.matmul
            pe.wait_ge(ld_tab, 16)

            def prepare_weights(half):
                pe.wait_ge(ld_W, 64 * (half + 1))
                pe.wait_ge(ld_A, 32)
                pe.wait_ge(pB_done, 2)
                for n in range(KD * half, KD * (half + 1)):
                    k, q = n // 2, n % 2
                    if n >= 2:
                        pe.wait_ge(prep_hi, n - 1)
                        pe.wait_ge(prep_lo, n - 1)
                    for a in range(2):
                        mm(fo_ps[q][:, :], A_sb[a][:, k * P:(k + 1) * P], pB[:, a, q * HALF:(q + 1) * HALF],
                           start=(a == 0), stop=False)
                    mm(fo_ps[q][:, :], ident, W_rows[k % 4][:, q * HALF:(q + 1) * HALF],
                       start=False, stop=True).then_inc(prep_full, 1)

            def slot(i, s):
                u = 2 * i + s
                v = u - 1
                if live(v, UNITS):
                    pe.wait_ge(top_step, TOP_STEPS * (v + 1))
                    for f in range(2):
                        if some(v):
                            pe.wait_ge(xw_evac, XW_FILLS * v + f - 1)
                        for t in range(TILES):
                            last = nc.tensor.transpose(xw_ps[f][:, t * P:(t + 1) * P],
                                                       prob[:, t, f * P:(f + 1) * P], ident)
                        last.then_inc(xw_full, 1)
                    for k, (c, f) in enumerate(((FC, 0), (FS, 1), (NC, 1), (NS, 0))):
                        pe.wait_ge(xw_evac, XW_FILLS * v + max(k + 1, f + 1))
                        mm(xw_ps[k % 2][:, :], tab[:, c:c + P], wfold[:, f, :],
                           start=True, stop=True).then_inc(xw_full, 1)
                j = u - 3
                if live(j, UNITS):
                    pe.wait_ge(xhat_done, j + 1)
                    pe.wait_ge(t_evac, most(T_FILLS * (u + 1), T_FILLS * UNITS))
                    if some(j):
                        pe.wait_ge(ft_lo, 2 * j)
                    for f in range(2):
                        for k in range(4):
                            last = nc.tensor.transpose(t_ps[f][:, k * P:(k + 1) * P],
                                                       xhat[:, (4 * f + k) * P:(4 * f + k + 1) * P], ident)
                        last.then_inc(ft_full, 1)
                    pe.wait_ge(x1_step, most(2 * (u - 1), 2 * UNITS))
                    if some(j):
                        pe.wait_ge(f_evac, 2 * j)
                    for k in range(KD):
                        if k % 4 == 0:
                            pe.wait_ge(ft_hi, 2 * j + k // 4 + 1)
                        for wt in (w_hi, w_lo):
                            for q in range(2):
                                mm(fo_ps[q][:, :], xT_hi[:, k, :], wt[:, k, q * HALF:(q + 1) * HALF],
                                   start=(k == 0 and wt is w_hi), stop=False)
                    pe.wait_ge(ft_lo, 2 * j + 2)
                    for q in range(2):
                        for k in range(KD):
                            last = mm(fo_ps[q][:, :], xT_lo[:, k, :], w_hi[:, k, q * HALF:(q + 1) * HALF],
                                      start=False, stop=(k == KD - 1))
                        last.then_inc(f_full, 1)
                if isinstance(u, int) and u in (0, 1):
                    prepare_weights(u)
                v = u + 1
                if live(v, UNITS):
                    pe.wait_ge(fold_step, FOLD_STEPS * (v + 1))
                    if live(j, UNITS):
                        pe.wait_ge(ft_lo, 2 * j + 2)
                    for k, (c, src) in enumerate(((FC, eq), (FS, oq), (FC, ev), (FS, ov), (NC, ov), (NS, ev))):
                        if k >= 2 or some(v):
                            pe.wait_ge(t_evac, T_FILLS * v + k - 1)
                        mm(t_ps[k % 2][:, :], tab[:, c:c + P], src[:, :], start=True, stop=True).then_inc(t_full, 1)
                v = u - 1
                if live(v, UNITS):
                    pe.wait_ge(p2_step, P2_STEPS * (v + 1))
                    pe.wait_ge(nyq2, v + 1)
                    if some(v):
                        pe.wait_ge(x1_step, 2 * v)
                    else:
                        pe.wait_ge(basis_ready, 1)
                        pe.wait_ge(prep_hi, 2 * KD)
                        pe.wait_ge(prep_lo, 2 * KD)
                    if live(j, UNITS):
                        pe.wait_ge(f_evac, 2 * j + 2)
                    for r in range(2):
                        for k, spec in enumerate((Wsp[:, 0, :], cyc_im[:, :], Wsp[:, 2, :], neg_im[:, :])):
                            c = OUT + k * L + r * P
                            last = mm(fo_ps[r][:, :], tab[:, c:c + P], spec, start=(k == 0), stop=(k == 3))
                        last.then_inc(o_full, 1)
                v = u + 1
                if live(v, UNITS):
                    pe.wait_ge(p1_step, P1_STEPS * (v + 1))
                    pe.wait_ge(nyq1, v + 1)
                    if some(v):
                        pe.wait_ge(c_evac, 2 * v)
                    for n in range(2):
                        for t in (2 * n, 2 * n + 1):
                            ps = c_ps[n][:, (t % 2) * L:(t % 2 + 1) * L]
                            mm(ps, Qc[:, t * P:(t + 1) * P], tab[:, CORR_C:CORR_C + L], start=True, stop=False)
                            last = mm(ps, corr_im[:, t * P:(t + 1) * P], tab[:, CORR_S:CORR_S + L],
                                      start=False, stop=True)
                        last.then_inc(c_full, 1)

            all_slots(pe, slot)

        @block.scalar
        def _(act):
            def prepare_weights(half):
                for n in range(KD * half, KD * (half + 1)):
                    k, q = n // 2, n % 2
                    act.wait_ge(prep_full, n + 1)
                    nc.scalar.activation(w_hi[:, k, q * HALF:(q + 1) * HALF], fo_ps[q][:, :],
                                         ACT.Copy, scale=g_t[:, 1:2]).then_inc(prep_hi, 1)

            act.wait_ge(ld_g, 32)
            nc.scalar.activation(g_t[:, :], g_in[:, :], ACT.Tanh).then_inc(g_ready, 1)
            act.preload_act_table_set("natural_log_exp_and_others")
            act.wait_ge(g_ready, 1)
            act.wait_ge(ld_tab, 16)
            nc.scalar.activation(tab[:, OUT:OUT + 4 * L], tab[:, OUT:OUT + 4 * L], ACT.Copy,
                                 scale=g_t[:, 0:1]).then_inc(basis_ready, 1)

            def expert_weights():
                act.wait_ge(ld_probs, 32)
                act.wait_ge(ld_B, 16)
                for a in range(2):
                    nc.scalar.activation(pB[:, a, :], pB[:, a, :], ACT.Copy, scale=pr[:, a:a + 1]
                                         ).then_inc(pB_done, 1)

            def slot(i, s):
                u = 2 * i + s
                if isinstance(u, int) and u == -2:
                    expert_weights()
                v = u - 1
                if live(v, UNITS):
                    for k in range(XW_FILLS):
                        act.wait_ge(xw_full, XW_FILLS * v + k + 1)
                        if k == 2 and some(v):
                            act.wait_ge(o_full, 2 * v)
                        dst = wfold[:, k, :] if k < 2 else Wsp[:, k - 2, :]
                        nc.scalar.activation(dst, xw_ps[k % 2][:, :], ACT.Copy).then_inc(xw_evac, 1)
                j = u - 3
                if live(j, UNITS):
                    for f in range(2):
                        act.wait_ge(ft_full, 2 * j + f + 1)
                        nc.scalar.activation(xT_hi[:, 4 * f:4 * f + 4, :],
                                             t_ps[f][:, :].rearrange("p (k n) -> p k n", k=4),
                                             ACT.Copy).then_inc(ft_hi, 1)
                if live(u, UNITS):
                    act.wait_ge(top_step, TOP_STEPS * u + 13)
                    nc.scalar.activation(top_exp[:, :, :], top_rel[:, :, :], ACT.Exp).then_inc(top_act, 1)
                    act.wait_ge(top_step, TOP_STEPS * u + 19)
                    nc.scalar.activation(log_sum[:, :], top_sum[:, :], ACT.Ln).then_inc(top_act, 1)
                    act.wait_ge(top_step, TOP_STEPS * u + 20)
                    for t in range(TILES):
                        nc.scalar.activation(prob[:, t, :], corr[:, t, :], ACT.Exp,
                                             bias=exp_bias[:, t:t + 1]).then_inc(exp_done, 1)
                if isinstance(u, int) and u in (0, 1):
                    prepare_weights(u)
                v = u + 1
                if live(v, UNITS):
                    h = 1 - s
                    for k in range(T_FILLS):
                        act.wait_ge(t_full, T_FILLS * v + k + 1)
                        if k == 0 and some(v):
                            act.wait_ge(c_full, 2 * v)
                        if k == 2 and some(v - 1):
                            act.wait_ge(p2_step, P2_STEPS * (v - 1))
                        dst = (Qc, Qs)[k][:, :] if k < 2 else V[:, h, k - 2, :]
                        nc.scalar.activation(dst, t_ps[k % 2][:, :], ACT.Copy).then_inc(t_evac, 1)
                w = u + 2
                if live(w, UNITS):
                    act.wait_ge(rs_step[0], RS_STEPS * (i + 2))
                    if some(w):
                        act.wait_ge(fold_step, FOLD_STEPS * w)
                    for r in range(2):
                        nc.scalar.activation(qh[:, r, :], x_half(i + 1, r, s), ACT.Identity,
                                             bias=shift[0][:, r:r + 1],
                                             scale=rstd[0][:, r:r + 1]).then_inc(qhat_done, 1)
                v = u + 1
                if live(v, UNITS):
                    for n in range(2):
                        act.wait_ge(c_full, 2 * v + n + 1)
                        nc.scalar.activation(corr[:, 2 * n:2 * n + 2, :],
                                             c_ps[n][:, :].rearrange("p (t l) -> p t l", t=2),
                                             ACT.Copy).then_inc(c_evac, 1)
                j = u - 2
                if live(j, UNITS):
                    act.wait_ge(rs_step[1], RS_STEPS * i)
                    if some(j):
                        act.wait_ge(ft_full, 2 * j)
                    nc.scalar.activation(xhat[:, :], x_tile(i - 1, s), ACT.Identity, bias=shift[1][:, s:s + 1],
                                         scale=rstd[1][:, s:s + 1]).then_inc(xhat_done, 1)

            all_slots(act, slot)

        @block.vector
        def _(dve):
            tt = nc.vector.tensor_tensor
            stt = nc.vector.scalar_tensor_tensor

            def layer_stats(b, n):
                step = ln_step[n]
                if some(b):
                    dve.wait_ge(rs_step[n], RS_STEPS * b)
                for r in range(2):
                    for c in range(2):
                        nc.vector.bn_stats(stats[n][:, r, c, :], x_half(b, r, c)).then_inc(step, 1)
                dve.wait_ge(step, LN_STEPS * b + 4)
                apart(dve, dve_turns)
                for r in range(2):
                    nc.vector.bn_aggr(mv[n][:, r, :], stats[n][:, r, :, :]).then_inc(step, 1)

            def slot(i, s):
                u = 2 * i + s
                base = TOP_STEPS * u
                if live(u, UNITS):
                    dve.wait_ge(c_evac, 2 * (u + 1))
                    apart(dve, dve_turns)
                    for t in range(TILES):
                        nc.vector.max(top[:, t, 0:8], corr[:, t, :]).then_inc(top_step, 1)
                    dve.wait_ge(top_step, base + 4)
                    apart(dve, dve_turns)
                    for t in range(TILES):
                        nc.vector.match_replace(left[:, t, :], top[:, t, 0:8], corr[:, t, :], GONE
                                                ).then_inc(top_step, 1)
                    dve.wait_ge(top_step, base + 8)
                    apart(dve, dve_turns)
                    for t in range(TILES):
                        nc.vector.max(top[:, t, 8:16], left[:, t, :]).then_inc(top_step, 1)
                    dve.wait_ge(top_step, base + 12)
                    tt(top_rel[:, :, :], top[:, :, 0:TOPK], top[:, :, 0:1].broadcast_to((P, TILES, TOPK)),
                       ALU.subtract).then_inc(top_step, 1)
                    nc.vector.memset(top[:, :, TOPK:16], GONE).then_inc(top_step, 1)
                    dve.wait_ge(top_step, base + 14)
                    apart(dve, dve_turns)
                    for t in range(TILES):
                        nc.vector.match_replace(left[:, t, :], top[:, t, 8:16], left[:, t, :], GONE
                                                ).then_inc(top_step, 1)
                j = u - 3
                if live(j, UNITS):
                    for f in range(2):
                        dve.wait_ge(ft_hi, 2 * j + f + 1)
                        tt(xT_lo[:, 4 * f:4 * f + 4, :], t_ps[f][:, :].rearrange("p (k n) -> p k n", k=4),
                           xT_hi[:, 4 * f:4 * f + 4, :].bitcast(F32), ALU.subtract).then_inc(ft_lo, 1)
                if live(u, UNITS):
                    dve.wait_ge(top_act, 2 * u + 1)
                    nc.vector.reduce_sum(top_sum[:, :], top_exp[:, :, :], mybir.AxisListType.X
                                         ).then_inc(top_step, 1)

                v = u - 1
                p2 = P2_STEPS * v
                h = 1 - s
                if live(v, UNITS):
                    nVc, nVs, nWc, nWs = V[:, h, 2, :], V[:, h, 3, :], Wsp[:, 2, :], Wsp[:, 3, :]
                    cVc, cVs, cWc, cWs = V[:, h, 0, :], V[:, h, 1, :], Wsp[:, 0, :], Wsp[:, 1, :]
                    dve.wait_ge(xw_evac, XW_FILLS * (v + 1))
                    dve.wait_ge(fix_step, FIX_STEPS * (v + 1))
                    dve.wait_ge(nyq1, most(u + 1, UNITS))
                    if some(v):
                        dve.wait_ge(o_full, 2 * v)
                    tt(prod[:, :], nVs, nWs, ALU.mult).then_inc(p2_step, 1)
                    tt(neg_im[:, :], nVc, nWs, ALU.mult).then_inc(p2_step, 1)
                if live(u, UNITS):
                    dve.wait_ge(top_act, 2 * u + 2)
                    stt(out=exp_bias[:, :], in0=log_sum[:, :], scalar=-1.0, in1=top[:, :, 0],
                        op0=ALU.mult, op1=ALU.subtract).then_inc(top_step, 1)
                if live(v, UNITS):
                    tt(cyc_im[:, :], cVc, cWs, ALU.mult).then_inc(p2_step, 1)
                    dve.wait_ge(p2_step, p2 + 2)
                    tt(nWs, nVs, nWc, ALU.mult).then_inc(p2_step, 1)
                    dve.wait_ge(p2_step, p2 + 4)
                    tt(nWc, nVc, nWc, ALU.mult).then_inc(p2_step, 1)
                    tt(neg_im[:, :], neg_im[:, :], nWs, ALU.subtract).then_inc(p2_step, 1)
                    dve.wait_ge(p2_step, p2 + 5)
                    tt(nWc, prod[:, :], nWc, ALU.add).then_inc(p2_step, 1)
                    dve.wait_ge(p2_step, p2 + 7)
                    tt(prod[:, :], cVs, cWs, ALU.mult).then_inc(p2_step, 1)
                    dve.wait_ge(p2_step, p2 + 8)
                    tt(cWs, cVs, cWc, ALU.mult).then_inc(p2_step, 1)
                    dve.wait_ge(p2_step, p2 + 9)
                    tt(cWc, cVc, cWc, ALU.mult).then_inc(p2_step, 1)
                    tt(cyc_im[:, :], cyc_im[:, :], cWs, ALU.subtract).then_inc(p2_step, 1)
                    dve.wait_ge(p2_step, p2 + 10)
                    stt(out=cWc, in0=prod[:, :], scalar=mask, in1=cWc, op0=ALU.mult, op1=ALU.add
                        ).then_inc(p2_step, 1)
                if live(u, UNITS):
                    for f in range(2):
                        dve.wait_ge(exp_done, TILES * u + 2 * f + 2)
                        stt(out=left[:, 2 * f:2 * f + 2, :], in0=left[:, 2 * f:2 * f + 2, :], scalar=0.95 * GONE,
                            in1=prob[:, 2 * f:2 * f + 2, :], op0=ALU.is_le, op1=ALU.mult).then_inc(top_step, 1)
                    dve.wait_ge(top_step, base + 22)
                    for f, op in enumerate((ALU.add, ALU.subtract)):
                        tt(prob[:, :, f * P:(f + 1) * P], left[:, :, 0:P], left[:, :, L - 1:P - 1:-1],
                           op).then_inc(top_step, 1)
                if live(j, UNITS):
                    b, r = (i - 2, 1) if s == 0 else (i - 1, 0)
                    dve.wait_ge(gb_added, j + 1)
                    for q in range(2):
                        dve.wait_ge(f_full, 2 * j + q + 1)
                        tt(x_half(b, r, q), x_half(b, r, q), fo_ps[q][:, :], ALU.add).then_inc(f_evac, 1)
                if isinstance(u, int) and u in (0, 1):
                    for n in range(KD * u, KD * (u + 1)):
                        k, q = n // 2, n % 2
                        dve.wait_ge(prep_hi, n + 1)
                        stt(out=w_lo[:, k, q * HALF:(q + 1) * HALF], in0=fo_ps[q][:, :],
                            scalar=g_t[:, 1:2], in1=w_hi[:, k, q * HALF:(q + 1) * HALF].bitcast(F32),
                            op0=ALU.mult, op1=ALU.subtract).then_inc(prep_lo, 1)
                if s == 0 and live(i + 1, BATCH):
                    dve.wait_ge(ld_x, 16 * (i + 2))
                    layer_stats(i + 1, 0)
                v = u + 1
                if live(v, UNITS):
                    p1 = P1_STEPS * v
                    Kc, Ks = V[:, h, 0, :], V[:, h, 1, :]
                    if isinstance(u, int) and u == -1:
                        dve.wait_ge(ld_tab, 16)
                    dve.wait_ge(t_evac, T_FILLS * v + 4)
                    if some(u):
                        dve.wait_ge(nyq2, u)
                    tt(prod[:, :], Qs[:, :], Ks, ALU.mult).then_inc(p1_step, 1)
                    tt(corr_im[:, :], Qc[:, :], Ks, ALU.mult).then_inc(p1_step, 1)
                    dve.wait_ge(p1_step, p1 + 1)
                    tt(Qs[:, :], Qs[:, :], Kc, ALU.mult).then_inc(p1_step, 1)
                    dve.wait_ge(p1_step, p1 + 2)
                    tt(Qc[:, :], Qc[:, :], Kc, ALU.mult).then_inc(p1_step, 1)
                    dve.wait_ge(p1_step, p1 + 3)
                    tt(corr_im[:, :], corr_im[:, :], Qs[:, :], ALU.subtract).then_inc(p1_step, 1)
                    dve.wait_ge(p1_step, p1 + 4)
                    stt(out=Qc[:, :], in0=prod[:, :], scalar=mask, in1=Qc[:, :], op0=ALU.mult, op1=ALU.add
                        ).then_inc(p1_step, 1)
                w = u + 2
                if live(w, UNITS):
                    if some(w):
                        dve.wait_ge(t_full, T_FILLS * w)
                    dve.wait_ge(ld_v, 16 * (i + 2))
                    kv = [vt[:, r, s * HALF:(s + 1) * HALF] for r in range(2)]
                    tt(ev[:, :], kv[0], kv[1], ALU.add).then_inc(fold_step, 1)
                    tt(ov[:, :], kv[0], kv[1], ALU.subtract).then_inc(fold_step, 1)
                    dve.wait_ge(qhat_done, 2 * (w + 1))
                    tt(eq[:, :], qh[:, 0, :], qh[:, 1, :], ALU.add).then_inc(fold_step, 1)
                    tt(oq[:, :], qh[:, 0, :], qh[:, 1, :], ALU.subtract).then_inc(fold_step, 1)
                v = u - 1
                if live(v, UNITS):
                    b = i - 1 if s == 0 else i
                    for r in range(2):
                        dve.wait_ge(o_full, 2 * v + r + 1)
                        tt(x_half(b, r, h), x_half(b, r, h), fo_ps[r][:, :], ALU.add).then_inc(x1_step, 1)
                if s == 0 and live(i - 1, BATCH):
                    dve.wait_ge(x1_step, 4 * i)
                    layer_stats(i - 1, 1)

            all_slots(dve, slot)

        @block.gpsimd
        def _(pool):
            ptt = nc.gpsimd.tensor_tensor
            for c, value in enumerate((-0.5, EPS, -1.0, float(L), 1.0)):
                nc.gpsimd.memset(consts[:, c, :], value).then_inc(consts_ready, 1)
            pool.wait_ge(consts_ready, 5)
            minus_half, eps, minus_one, steps = (consts[:, c, :] for c in range(4))
            one_row = consts[0:1, 4, 0:1].broadcast_to((1, HALF))

            def row_scales(b, n):
                step, done = rs_step[n], RS_STEPS * b
                pool.wait_ge(ln_step[n], LN_STEPS * (b + 1))
                ptt(var_eps[n][:, :], mv[n][:, :, 1], eps, ALU.add).then_inc(step, 1)
                pool.wait_ge(step, done + 1)
                ptt(rstd[n][:, :], var_eps[n][:, :], minus_half, ALU.pow).then_inc(step, 1)
                pool.wait_ge(step, done + 2)
                ptt(shift[n][:, :], mv[n][:, :, 0], rstd[n][:, :], ALU.mult).then_inc(step, 1)
                pool.wait_ge(step, done + 3)
                ptt(shift[n][:, :], shift[n][:, :], minus_one, ALU.mult).then_inc(step, 1)

            def slot(i, s):
                u = 2 * i + s
                v = u - 1
                if live(v, UNITS):
                    pool.wait_ge(p2_step, P2_STEPS * (v + 1))
                    ptt(cyc_im[0:1, :], prod[0:1, :], one_row, ALU.mult).then_inc(nyq2, 1)
                if s == 0 and live(i + 1, BATCH):
                    if some(i + 1):
                        pool.wait_ge(qhat_done, 4 * (i + 1))
                    row_scales(i + 1, 0)
                v = u + 1
                if live(v, UNITS):
                    h = 1 - s
                    b = i if s == 0 else i + 1
                    cols = slice(h * HALF, (h + 1) * HALF)
                    fix = FIX_STEPS * v
                    pool.wait_ge(p1_step, P1_STEPS * (v + 1))
                    ptt(corr_im[0:1, :], prod[0:1, :], one_row, ALU.mult).then_inc(nyq1, 1)
                    pool.wait_ge(ld_vl, 16 * (b + 1))
                    ptt(vl[0:1, cols], vl[0:1, cols], steps[0:1, 0:1].broadcast_to((1, HALF)), ALU.mult).then_inc(fix_step, 1)
                    pool.wait_ge(fix_step, fix + 1)
                    ptt(V[0:1, h, 0, :], V[0:1, h, 0, :], vl[0:1, cols], ALU.add).then_inc(fix_step, 1)
                    pool.wait_ge(fix_step, fix + 2)
                    ptt(vl[:, cols], vl[:, cols], tab[:, NSIN:NSIN + 1].broadcast_to((P, HALF)), ALU.mult).then_inc(fix_step, 1)
                    pool.wait_ge(fix_step, fix + 3)
                    pool.wait_ge(t_evac, T_FILLS * (v + 1))
                    ptt(V[:, h, 3, :], V[:, h, 3, :], vl[:, cols], ALU.add).then_inc(fix_step, 1)
                if s == 0 and live(i - 1, BATCH):
                    if some(i - 1):
                        pool.wait_ge(xhat_done, 2 * (i - 1))
                    row_scales(i - 1, 1)
                j = u - 2
                if live(j, UNITS):
                    if isinstance(j, int) and j == 0:
                        pool.wait_ge(ld_bias, 16)
                        pool.wait_ge(g_ready, 1)
                        ptt(gbias[:, :], gbias[:, :], g_t[:, 1:2].broadcast_to((P, D)), ALU.mult).then_inc(gbias_ready, 1)
                        pool.wait_ge(gbias_ready, 1)
                    pool.wait_ge(xhat_done, j + 1)
                    ptt(x_tile(i - 1, s), x_tile(i - 1, s), gbias[:, :], ALU.add).then_inc(gb_added, 1)

            all_slots(pool, slot)


def constants():
    import numpy as np
    f = np.arange(P)
    n = f + 0.5
    sine_f = f.copy()
    sine_f[0] = P
    odd = (2 * f + 1) * np.pi / L
    t = np.arange(L)
    rows = np.concatenate([t[:P], t[:P - 1:-1]])
    cos, sin = 2 * np.cos(2 * np.pi * np.outer(f, t) / L), -2 * np.sin(2 * np.pi * np.outer(f, t) / L)
    cos[0], sin[0] = 1.0, (-1.0) ** t
    scale = 1.0 / L
    parts = [
        np.cos(2 * np.pi * np.outer(n, f) / L), np.sin(2 * np.pi * np.outer(n, sine_f) / L),
        np.cos(np.outer(n, odd)), np.sin(np.outer(n, odd)),
        cos * scale, sin * scale,
        cos[:, rows] * scale / 2, sin[:, rows] * scale / 2,
        np.cos(np.outer(odd, rows)) * scale, -np.sin(np.outer(odd, rows)) * scale,
        np.eye(P), (f > 0)[:, None], (-1.0 / np.sin(odd / 2) / np.where(f == 0, L, 1))[:, None],
    ]
    return np.ascontiguousarray(np.concatenate(parts, axis=1).astype(np.float32))


def kernel(**inputs):
    import numpy as np
    import concourse.bacc as bacc
    from concourse.bass_utils import run_bass_kernel_spmd

    def paired(a):
        return np.ascontiguousarray(np.stack([a[:, :P], a[:, :P - 1:-1]], axis=2))

    data = {k: np.asarray(v) for k, v in inputs.items()}
    arrays = {
        "x": paired(data["x"]), "ctx": paired(data["ctx_4096"]),
        "v_last": np.ascontiguousarray(data["ctx_4096"][:, L - 1, :]),
        "g_xattn": data["g_xattn"], "g_ffn": data["g_ffn"], "W": data["L0_ffn_W"].T, "b": data["L0_ffn_b"],
        "A": data["L0_ffn_A"],
        "B": data["L0_ffn_B"].transpose(0, 2, 1).reshape(E * R, D), "probs": data["L0_ffn_probs"], "table": constants(),
    }
    arrays = {f"in_{k}": np.ascontiguousarray(v) for k, v in arrays.items()}
    nc = bacc.Bacc("TRN2", target_bir_lowering=False, num_devices=1)
    args = [nc.dram_tensor(k, v.shape, mybir.dt.from_np(v.dtype), kind="ExternalInput").ap()
            for k, v in arrays.items()]
    out = nc.dram_tensor("out", (BATCH, 2, P, D), F32, kind="ExternalOutput").ap()
    build(nc, *args, out)
    r = run_bass_kernel_spmd(nc, [arrays], core_ids=[0])
    got = r.results[0]["out"]
    return np.concatenate([got[:, 0], got[:, 1, ::-1]], axis=1)
```

```python
from contextlib import ExitStack

import concourse.bass as bass
from concourse import mybir

F32 = mybir.dt.float32
F32R = mybir.dt.float32r
BF16 = mybir.dt.bfloat16
ALU = mybir.AluOpType
ACT = mybir.ActivationFunctionType

P = 128
BATCH, L, D = 8, 256, 1024
HALF = D // 2
UNITS = 2 * BATCH
TILES = HALF // P
KD = D // P
E, R = 16, 16
TOPK = 11
GONE = -3.0e38
EPS = 1e-5

FC, FS, NC, NS, IDENT = 0, P, 2 * P, 3 * P, 4 * P
MASK, NSIN = IDENT + P, IDENT + P + 1
TABLE = NSIN + 1
CORR, OUT = 0, 2 * L
INVERSE = OUT + 4 * L

T_FILLS = 6
XW_FILLS = 5
P1_STEPS = 4
P2_STEPS = 5
OS_HI_STEPS = 3
TOP_STEPS = 23
RS_STEPS = (5, 4)
FIX_STEPS = 4
RING = 4
PREPARED_PE = {(-1, "scores"): (0, 2), (-1, "end"): (2, 4), (0, "values"): (4, 8), (0, "scores"): (8, 10),
               (0, "end"): (10, 11), (1, "values"): (11, 16)}
PREPARED_ACT = {(-1, "scores"): (0, 2), (0, "softmax"): (2, 6), (0, "values"): (6, 7), (0, "scores"): (7, 9), (0, "end"): (9, 11),
                (1, "softmax"): (11, 16)}
PREPARED_DVE = {(-1, "end"): (0, 2), (0, "max"): (2, 3), (0, "replaced"): (3, 4), (0, "max again"): (4, 5),
                (0, "replaced again"): (5, 6), (0, "weights"): (6, 7), (0, "scores"): (7, 9), (0, "end"): (9, 11),
                (1, "max"): (11, 12), (1, "replaced"): (12, 13), (1, "max again"): (13, 14),
                (1, "replaced again"): (14, 16)}


def live(v, n):
    return not isinstance(v, int) or 0 <= v < n


def some(v):
    return not isinstance(v, int) or v > 0


def most(v, n):
    return min(v, n) if isinstance(v, int) else v


def blocks(prepared, slot, place):
    return range(*prepared.get((slot, place), (0, 0))) if isinstance(slot, int) else ()


def apart(eng, turns):
    eng.sem_inc(turns, 1)


def build(nc, x, ctx_kv, v_last, g_attn, g_ffn, W, bias, A, B, probs, table, inverse, out):
    with ExitStack() as ctx:
        def sb(name, shape, dt=F32):
            return ctx.enter_context(nc.sbuf_tensor(name, shape, dt))

        def sem(name):
            return ctx.enter_context(nc.semaphore(name))

        def whole_and_split(name, shape):
            with nc.sbuf_tensor(name, shape, F32) as whole:
                pass
            return whole, sb(f"{name}_r", shape, F32R)

        tab = sb("tab", [P, TABLE])
        inv_hi, inv_lo = sb("inv_hi", [P, INVERSE], F32R), sb("inv_lo", [P, INVERSE], F32R)
        w_hi = sb("w_hi", [P, KD, D], F32R)
        w_lo = sb("w_lo", [P, KD, D], F32R)
        xr = sb("xr", [P, RING, 2, D])
        qh = sb("qh", [P, 2, HALF])
        vt = sb("vt", [P, 2, D])
        vl = sb("vl", [P, D])
        eq, oq, ev, ov = (sb(n, [P, HALF]) for n in ("eq", "oq", "ev", "ov"))
        QX, QX_r = whole_and_split("QX", [P, 4, HALF])
        WX, WX_r = whole_and_split("WX", [P, 8, HALF])
        Q, Q_cross = QX[:, 0:2, :], QX[:, 2:4, :]
        Wsp, W_cross = WX[:, 0:4, :], WX[:, 4:8, :]
        V = sb("V", [P, 2, 4, HALF])
        wfold = sb("wfold", [P, 2, HALF])
        corr = sb("corr", [P, TILES, L])
        left = sb("left", [P, TILES, L])
        prob = sb("prob", [P, TILES, L])
        top = sb("top", [P, TILES, 16])
        top_rel = sb("top_rel", [P, TILES, TOPK])
        top_exp = sb("top_exp", [P, TILES, TOPK])
        top_sum, log_sum, exp_bias = (sb(n, [P, TILES]) for n in ("top_sum", "log_sum", "exp_bias"))
        xhat = sb("xhat", [P, D])
        xT_hi = sb("xT_hi", [P, KD, P], F32R)
        xT_lo = sb("xT_lo", [P, KD, P], F32R)
        gbias = sb("gbias", [P, D])
        row_sum, row_sq, minus_mean = (sb(n, [P, 2]) for n in ("row_sum", "row_sq", "minus_mean"))
        stats, mv = sb("stats", [P, 2, 2, 6]), sb("mv", [P, 2, 2])
        var_eps = [sb(f"var_eps{n}", [P, 2]) for n in (1, 2)]
        rstd = [sb(f"rstd{n}", [P, 2]) for n in (1, 2)]
        shift = [sb(f"shift{n}", [P, 2]) for n in (1, 2)]
        consts = sb("consts", [P, 7, 2])
        g_in, g_t = sb("g_in", [P, 2]), sb("g_t", [P, 2])
        pr = sb("pr", [P, 2])

        t_ps, xw_ps, c_ps, fo_ps = (ctx.enter_context(nc.psum_tensor(n, [P, 2, 512], F32))
                                    for n in ("t_ps", "xw_ps", "c_ps", "fo_ps"))

        pB = xr[:, 3, :, :]
        A_sb = [xhat, gbias]
        spare = [xr[:, 2, :, :].rearrange("p r d -> p (r d)")
                 ] + [WX[:, 4 * a:4 * a + 4, :].rearrange("p k n -> p (k n)") for a in range(2)]
        inv_corr = corr[:, 0:2, :].rearrange("p t l -> p (t l)")
        inv_out = prob[:, :, :].rearrange("p t l -> p (t l)")
        W_rows = [spare[k // 2 % 3][:, k % 2 * D:(k % 2 + 1) * D] for k in range(KD)]

        ident = tab[:, IDENT:IDENT + P]
        mask = tab[:, MASK:MASK + 1]

        ld_tab, ld_x, ld_v, ld_vl, ld_g = (sem(n) for n in ("ld_tab", "ld_x", "ld_v", "ld_vl", "ld_g"))
        ld_B, ld_A, ld_probs, ld_bias = (sem(n) for n in ("ld_B", "ld_A", "ld_probs", "ld_bias"))
        ld_W = [sem(f"ld_W{k}") for k in range(KD)]
        ld_inv, inv_hi_done, inv_lo_done = (sem(n) for n in ("ld_inv", "inv_hi_done", "inv_lo_done"))
        cs_hi, cs_lo, os_hi, os_lo = (sem(n) for n in ("cs_hi", "cs_lo", "os_hi", "os_lo"))
        st_out = [sem("st_lo"), sem("st_hi")]
        g_ready, gbias_ready, consts_ready = (sem(n) for n in ("g_ready", "gbias_ready", "consts_ready"))
        pB_done, prep_full, prep_sum, prep_hi, prep_lo = (sem(n) for n in ("pB_done", "prep_full", "prep_sum",
                                                                          "prep_hi", "prep_lo"))
        xw_full, xw_evac, t_full, t_evac = (sem(n) for n in ("xw_full", "xw_evac", "t_full", "t_evac"))
        ft_full, ft_hi, ft_lo, f_full, f_evac = (sem(n) for n in ("ft_full", "ft_hi", "ft_lo", "f_full", "f_evac"))
        o_full, x1_step, c_full, c_evac = (sem(n) for n in ("o_full", "x1_step", "c_full", "c_evac"))
        top_step, top_act, exp_done = (sem(n) for n in ("top_step", "top_act", "exp_done"))
        p1_step, p2_step, nyq1, nyq2, fix_step = (sem(n) for n in ("p1_step", "p2_step", "nyq1", "nyq2", "fix_step"))
        sum_done, sq_done, stats_done, mv_done = (sem(n) for n in ("sum_done", "sq_done", "stats_done", "mv_done"))
        rs_step = [sem("rs1_step"), sem("rs2_step")]
        qhat_done, q_fold, kv_fold, xhat_done, gb_added = (sem(n) for n in ("qhat_done", "q_fold", "kv_fold",
                                                                           "xhat_done", "gb_added"))
        act_turns, dve_turns, sp_turns = (sem(n) for n in ("act_turns", "dve_turns", "sp_turns"))
        block = ctx.enter_context(nc.Block())

        def x_tile(b, r):
            return xr[:, b & (RING - 1), r, :]

        def x_half(b, r, h):
            return xr[:, b & (RING - 1), r, h * HALF:(h + 1) * HALF]

        def all_slots(eng, slot):
            for i in (-1, 0, 1):
                slot(i, 0)
                slot(i, 1)
            with eng.Fori(2, 7) as i:
                slot(i, 0)
                slot(i, 1)
            for i in (7, 8, 9):
                slot(i, 0)
                slot(i, 1)

        @block.sync
        def _(sp):
            sp.dma_start(xr[:, 0, :, :], x[0]).then_inc(ld_x, 16)
            sp.dma_start(tab[:, :], table).then_inc(ld_tab, 16)
            sp.dma_start(vt[:, :, :], ctx_kv[0]).then_inc(ld_v, 16)
            sp.dma_start(g_in[:, 0:1], g_attn.partition_broadcast(P)).then_inc(ld_g, 16)
            sp.dma_start(g_in[:, 1:2], g_ffn.partition_broadcast(P)).then_inc(ld_g, 16)
            sp.dma_start(vl[:, :], v_last[0].partition_broadcast(P)).then_inc(ld_vl, 16)
            for q in range(2):
                sp.dma_start(pr[:, q:q + 1],
                             probs[q * 8:(q + 1) * 8].unsqueeze(1).broadcast_to((8, R)).unsqueeze(2)
                             ).then_inc(ld_probs, 16)
            sp.dma_start(pB, B.rearrange("(a p) o -> p a o", p=P)).then_inc(ld_B, 16)
            for q in range(2):
                sp.dma_start(A_sb[q][:, :], A.rearrange("e r d -> (e r) d")[q * P:(q + 1) * P]).then_inc(ld_A, 16)
            sp.dma_start(inv_corr, inverse[:, CORR:OUT]).then_inc(ld_inv, 16)
            sp.dma_start(inv_out, inverse[:, OUT:INVERSE]).then_inc(ld_inv, 16)
            for k in range(6):
                sp.dma_start(W_rows[k], W[k * P:(k + 1) * P]).then_inc(ld_W[k], 16)
            sp.wait_ge(ld_x, 16)
            sp.dma_start(xr[:, 1, :, :], x[1]).then_inc(ld_x, 16)
            sp.wait_ge(kv_fold, 4)
            sp.wait_ge(ld_v, 16)
            sp.dma_start(vt[:, :, :], ctx_kv[1]).then_inc(ld_v, 16)
            for k in (6, 7):
                sp.wait_ge(prep_lo, 2 * (k - 5))
                sp.dma_start(W_rows[k], W[k * P:(k + 1) * P]).then_inc(ld_W[k], 16)

            def body(i):
                if live(i - 2, BATCH):
                    sp.wait_ge(f_evac, 2 * (i - 2) + 2)
                    apart(sp, sp_turns)
                    sp.dma_start(out[i - 2, 1], x_tile(i - 2, 1)).then_inc(st_out[1], 16)
                if live(i + 1, BATCH):
                    sp.wait_ge(fix_step, FIX_STEPS * (2 * i + 2))
                    sp.wait_ge(ld_vl, 16 * (i + 1))
                    sp.dma_start(vl[:, :], v_last[i + 1].partition_broadcast(P)).then_inc(ld_vl, 16)
                if live(i - 1, BATCH):
                    sp.wait_ge(f_evac, 2 * (i - 1) + 1)
                    apart(sp, sp_turns)
                    sp.dma_start(out[i - 1, 0], x_tile(i - 1, 0)).then_inc(st_out[0], 16)
                if live(i + 2, BATCH):
                    sp.wait_ge(kv_fold, 4 * (i + 2))
                    apart(sp, sp_turns)
                    sp.wait_ge(ld_v, 16 * (i + 2))
                    sp.dma_start(vt[:, :, :], ctx_kv[i + 2]).then_inc(ld_v, 16)
                    if not isinstance(i, int) or i >= 2:
                        for r in range(2):
                            sp.wait_ge(st_out[r], 16 * (i - 1))
                    else:
                        sp.wait_ge(prep_lo, 2 * KD)
                    sp.wait_ge(ld_x, 16 * (i + 2))
                    apart(sp, sp_turns)
                    sp.dma_start(xr[:, (i + 2) & (RING - 1), :, :], x[i + 2]).then_inc(ld_x, 16)

            body(0)
            sp.dma_start(gbias[:, :], bias.partition_broadcast(P)).then_inc(ld_bias, 16)
            body(1)
            with sp.Fori(2, 6) as i:
                body(i)
            for i in (6, 7, 8, 9):
                body(i)
            for r in range(2):
                sp.wait_ge(st_out[r], 16 * BATCH)

        @block.tensor
        def _(pe):
            mm = nc.tensor.matmul
            pe.wait_ge(ld_tab, 16)

            def prepare_weights(u, place):
                for n in blocks(PREPARED_PE, u, place):
                    k, q = n // 2, n % 2
                    cols = slice(q * HALF, (q + 1) * HALF)
                    if n == 0:
                        pe.wait_ge(ld_A, 32)
                        pe.wait_ge(pB_done, 2)
                    if n >= 2:
                        pe.wait_ge(prep_sum, n - 1)
                    for a in range(2):
                        last = mm(fo_ps[:, q, :], A_sb[a][:, k * P:(k + 1) * P], pB[:, a, cols],
                                  start=(a == 0), stop=(a == 1))
                    last.then_inc(prep_full, 1)

            def transform(v, fills):
                for k in fills:
                    c, src = ((FC, eq), (FS, oq), (FC, ev), (FS, ov), (NC, ov), (NS, ev))[k]
                    if k >= 2 or some(v):
                        pe.wait_ge(t_evac, T_FILLS * v + k - 1)
                    mm(t_ps[:, k % 2, :], tab[:, c:c + P], src[:, :], start=True, stop=True).then_inc(t_full, 1)

            def slot(i, s):
                u = 2 * i + s
                v = u - 1
                if live(v, UNITS):
                    pe.wait_ge(top_step, TOP_STEPS * (v + 1))
                    if some(v):
                        pe.wait_ge(xw_evac, XW_FILLS * v)
                    for f in range(2):
                        for t in range(TILES):
                            last = nc.tensor.transpose(xw_ps[:, f, t * P:(t + 1) * P],
                                                       prob[:, t, f * P:(f + 1) * P], ident)
                    last.then_inc(xw_full, 1)
                j = u - 3
                if live(u + 1, UNITS):
                    if some(j) and live(j, UNITS):
                        pe.wait_ge(ft_lo, j)
                    pe.wait_ge(q_fold, 2 * (u + 2))
                    transform(u + 1, (0, 1))
                for f in range(2):
                    if live(v, UNITS):
                        for k, (c, fold) in list(enumerate(((FC, 0), (FS, 1), (NC, 1), (NS, 0))))[2 * f:2 * f + 2]:
                            pe.wait_ge(xw_evac, XW_FILLS * v + max(k, 1))
                            mm(xw_ps[:, k % 2, :], tab[:, c:c + P], wfold[:, fold, :],
                               start=True, stop=True).then_inc(xw_full, 1)
                    if live(j, UNITS):
                        if f == 0:
                            pe.wait_ge(xhat_done, j + 1)
                            pe.wait_ge(t_evac, most(T_FILLS * (u + 1) + 2, T_FILLS * UNITS))
                            if some(j):
                                pe.wait_ge(ft_lo, j)
                        for k in range(4):
                            last = nc.tensor.transpose(t_ps[:, f, k * P:(k + 1) * P],
                                                       xhat[:, (4 * f + k) * P:(4 * f + k + 1) * P], ident)
                        last.then_inc(ft_full, 1)
                if live(j, UNITS):
                    pe.wait_ge(x1_step, most(u - 1, UNITS))
                    if some(j):
                        pe.wait_ge(f_evac, j)
                    for k in range(KD):
                        if k % 4 == 0:
                            pe.wait_ge(ft_hi, 2 * j + k // 4 + 1)
                        for wt in (w_hi, w_lo):
                            for q in range(2):
                                mm(fo_ps[:, q, :], xT_hi[:, k, :], wt[:, k, q * HALF:(q + 1) * HALF],
                                   start=(k == 0 and wt is w_hi), stop=False)
                    pe.wait_ge(ft_lo, j + 1)
                    for q in range(2):
                        for k in range(KD):
                            last = mm(fo_ps[:, q, :], xT_lo[:, k, :], w_hi[:, k, q * HALF:(q + 1) * HALF],
                                      start=False, stop=(k == KD - 1))
                    last.then_inc(f_full, 1)
                prepare_weights(u, "values")
                v = u + 1
                if live(v, UNITS):
                    pe.wait_ge(kv_fold, 2 * (v + 1))
                    if live(j, UNITS):
                        pe.wait_ge(ft_lo, j + 1)
                    transform(v, (2, 3, 4, 5))
                v = u - 1
                if live(v, UNITS):
                    pe.wait_ge(os_hi, OS_HI_STEPS * (v + 1))
                    if some(v):
                        pe.wait_ge(x1_step, v)
                    else:
                        pe.wait_ge(inv_hi_done, 2)
                        pe.wait_ge(inv_lo_done, 2)
                        pe.wait_ge(prep_sum, 2 * KD)
                    if live(j, UNITS):
                        pe.wait_ge(f_evac, j + 1)
                    planes = (0, 4, 2, 6)
                    for r in range(2):
                        for k, plane in enumerate(planes):
                            c = OUT + k * L + r * P
                            for basis in (inv_hi, inv_lo):
                                mm(fo_ps[:, r, :], basis[:, c:c + P], WX_r[:, plane + 1, :],
                                   start=(k == 0 and basis is inv_hi), stop=False)
                    pe.wait_ge(os_lo, 2 * (v + 1))
                    for r in range(2):
                        for k, plane in enumerate(planes):
                            c = OUT + k * L + r * P
                            last = mm(fo_ps[:, r, :], inv_hi[:, c:c + P], WX_r[:, plane, :],
                                      start=False, stop=(k == 3))
                    last.then_inc(o_full, 1)
                prepare_weights(u, "scores")
                v = u + 1
                if live(v, UNITS):
                    if isinstance(u, int) and u == -1:
                        pe.wait_ge(inv_hi_done, 1)
                        pe.wait_ge(inv_lo_done, 1)
                    pe.wait_ge(cs_lo, v + 1)
                    if some(v):
                        pe.wait_ge(c_evac, 2 * v)
                    for n in range(2):
                        for t in (2 * n, 2 * n + 1):
                            ps = c_ps[:, n, (t % 2) * L:(t % 2 + 1) * L]
                            cols = slice(t * P, (t + 1) * P)
                            for part in range(2):
                                basis = slice(CORR + part * L, CORR + (part + 1) * L)
                                hi, lo = QX_r[:, 2 * part + 1, cols], QX_r[:, 2 * part, cols]
                                mm(ps, hi, inv_hi[:, basis], start=(part == 0), stop=False)
                                mm(ps, hi, inv_lo[:, basis], start=False, stop=False)
                                last = mm(ps, lo, inv_hi[:, basis], start=False, stop=(part == 1))
                        last.then_inc(c_full, 1)
                prepare_weights(u, "end")

            all_slots(pe, slot)

        @block.scalar
        def _(act):
            def prepare_weights(u, place):
                for n in blocks(PREPARED_ACT, u, place):
                    k, q = n // 2, n % 2
                    cols = slice(q * HALF, (q + 1) * HALF)
                    act.wait_ge(prep_sum, n + 1)
                    nc.scalar.activation(w_hi[:, k, cols], W_rows[k][:, cols], ACT.Copy, scale=g_t[:, 1:2]
                                         ).then_inc(prep_hi, 1)

            def gates():
                act.wait_ge(ld_g, 32)
                nc.scalar.activation(g_t[:, :], g_in[:, :], ACT.Tanh).then_inc(g_ready, 1)
                act.preload_act_table_set("natural_log_exp_and_others")

            def inverse_table():
                act.wait_ge(ld_inv, 32)
                nc.scalar.activation(inv_hi[:, CORR:OUT], inv_corr, ACT.Copy).then_inc(inv_hi_done, 1)
                act.wait_ge(g_ready, 1)
                nc.scalar.activation(inv_hi[:, OUT:INVERSE], inv_out, ACT.Copy, scale=g_t[:, 0:1]
                                     ).then_inc(inv_hi_done, 1)

            def normalize(r, b, j):
                act.wait_ge(rs_step[1], RS_STEPS[1] * (b + 1))
                if some(j):
                    act.wait_ge(ft_full, 2 * j)
                apart(act, act_turns)
                nc.scalar.activation(xhat[:, :], x_tile(b, r), ACT.Identity, bias=shift[1][:, r:r + 1],
                                     scale=rstd[1][:, r:r + 1]).then_inc(xhat_done, 1)

            def copy_spectra(v, fills, h):
                for k in fills:
                    act.wait_ge(t_full, T_FILLS * v + k + 1)
                    if k == 0 and some(v):
                        act.wait_ge(c_full, 2 * v)
                    if k == 2 and some(v - 1):
                        act.wait_ge(p2_step, P2_STEPS * (v - 2) + 2)
                    dst = Q[:, k, :] if k < 2 else V[:, h, k - 2, :]
                    nc.scalar.activation(dst, t_ps[:, k % 2, :], ACT.Copy).then_inc(t_evac, 1)

            scrap = qh[:, :, :].bitcast(BF16)

            def row_sums(i):
                act.wait_ge(ld_x, 16 * (i + 2))
                if some(i + 1):
                    act.wait_ge(q_fold, 4 * (i + 1))
                    act.wait_ge(rs_step[0], RS_STEPS[0] * (i + 1))
                apart(act, act_turns)
                for r in range(2):
                    nc.scalar.activation(scrap[:, r, :], x_tile(i + 1, r), ACT.Identity,
                                         accum_out=row_sum[:, r:r + 1]).then_inc(sum_done, 1)

            def row_squares(i):
                act.wait_ge(rs_step[0], RS_STEPS[0] * (i + 1) + 1)
                apart(act, act_turns)
                for r in range(2):
                    nc.scalar.activation(scrap[:, r, :], x_tile(i + 1, r), ACT.Square,
                                         bias=minus_mean[:, r:r + 1],
                                         accum_out=row_sq[:, r:r + 1]).then_inc(sq_done, 1)

            def slot(i, s):
                u = 2 * i + s
                if isinstance(u, int) and u == -1:
                    gates()
                    inverse_table()
                v = u - 1
                if live(v, UNITS):
                    act.wait_ge(xw_full, XW_FILLS * v + 1)
                    nc.scalar.activation(wfold[:, :, :], xw_ps[:, :, :], ACT.Copy).then_inc(xw_evac, 1)
                j = u - 3
                if live(j, UNITS):
                    b, r = (i - 2, 1) if s == 0 else (i - 1, 0)
                    normalize(r, b, j)
                if live(u + 1, UNITS):
                    copy_spectra(u + 1, (0, 1), 1 - s)

                def copy_weight_spectra(fills):
                    for k in fills:
                        act.wait_ge(xw_full, XW_FILLS * v + k + 2)
                        if k == 0 and some(v):
                            act.wait_ge(o_full, v)
                        elif k == 0:
                            act.wait_ge(prep_lo, 8)
                        nc.scalar.activation(Wsp[:, k, :], xw_ps[:, k % 2, :], ACT.Copy).then_inc(xw_evac, 1)

                for f in range(2):
                    if live(v, UNITS):
                        copy_weight_spectra((2 * f, 2 * f + 1))
                    if live(j, UNITS):
                        act.wait_ge(ft_full, 2 * j + f + 1)
                        nc.scalar.activation(xT_hi[:, 4 * f:4 * f + 4, :],
                                             t_ps[:, f, :].rearrange("p (k n) -> p k n", k=4),
                                             ACT.Copy).then_inc(ft_hi, 1)
                prepare_weights(u, "softmax")
                if live(u, UNITS):
                    act.wait_ge(top_step, TOP_STEPS * u + 13)
                    nc.scalar.activation(top_exp[:, :, :], top_rel[:, :, :], ACT.Exp).then_inc(top_act, 1)
                    act.wait_ge(top_step, TOP_STEPS * u + 19)
                    nc.scalar.activation(log_sum[:, :], top_sum[:, :], ACT.Ln).then_inc(top_act, 1)
                    act.wait_ge(top_step, TOP_STEPS * u + 20)
                    for t in range(TILES):
                        nc.scalar.activation(prob[:, t, :], corr[:, t, :], ACT.Exp,
                                             bias=exp_bias[:, t:t + 1]).then_inc(exp_done, 1)
                if s == 0 and live(i + 1, BATCH):
                    row_sums(i)
                v = u - 1
                if live(v, UNITS):
                    act.wait_ge(p2_step, P2_STEPS * v + 3)
                    nc.scalar.activation(WX_r[:, 3, :], WX[:, 2, :], ACT.Copy).then_inc(os_hi, 1)
                    act.wait_ge(p2_step, P2_STEPS * (v + 1))
                    nc.scalar.activation(W_cross[0:1, 0, :], Wsp[0:1, 1, :], ACT.Copy).then_inc(nyq2, 1)
                    act.wait_ge(nyq2, v + 1)
                    nc.scalar.activation(WX_r[:, 5:8:2, :], WX[:, 4:8:2, :], ACT.Copy).then_inc(os_hi, 1)
                    nc.scalar.activation(WX_r[:, 1, :], WX[:, 0, :], ACT.Copy).then_inc(os_hi, 1)
                prepare_weights(u, "values")
                if live(u + 1, UNITS):
                    copy_spectra(u + 1, (2, 3, 4, 5), 1 - s)
                if s == 0 and live(i + 1, BATCH):
                    row_squares(i)
                v = u + 1
                if live(v, UNITS):
                    act.wait_ge(p1_step, P1_STEPS * (v + 1))
                    nc.scalar.activation(Q_cross[0:1, 0, :], Q[0:1, 1, :], ACT.Copy).then_inc(nyq1, 1)
                    act.wait_ge(nyq1, v + 1)
                    nc.scalar.activation(QX_r[:, 1::2, :], QX[:, 0::2, :], ACT.Copy).then_inc(cs_hi, 1)
                w = u + 2
                if live(w, UNITS):
                    act.wait_ge(rs_step[0], RS_STEPS[0] * (i + 2))
                    if some(w):
                        act.wait_ge(q_fold, 2 * w)
                    apart(act, act_turns)
                    for r in range(2):
                        nc.scalar.activation(qh[:, r, :], x_half(i + 1, r, s), ACT.Identity,
                                             bias=shift[0][:, r:r + 1],
                                             scale=rstd[0][:, r:r + 1]).then_inc(qhat_done, 1)
                prepare_weights(u, "scores")
                if live(v, UNITS):
                    for n in range(2):
                        act.wait_ge(c_full, 2 * v + n + 1)
                        nc.scalar.activation(corr[:, 2 * n:2 * n + 2, :],
                                             c_ps[:, n, :].rearrange("p (t l) -> p t l", t=2),
                                             ACT.Copy).then_inc(c_evac, 1)
                prepare_weights(u, "end")

            all_slots(act, slot)

        @block.vector
        def _(dve):
            tt = nc.vector.tensor_tensor
            stt = nc.vector.scalar_tensor_tensor

            def expert_weights():
                dve.wait_ge(ld_probs, 32)
                dve.wait_ge(ld_B, 16)
                for a in range(2):
                    tt(pB[:, a, :], pB[:, a, :], pr[:, a:a + 1].broadcast_to((P, D)), ALU.mult
                       ).then_inc(pB_done, 1)

            def prepare_weights(u, place):
                for n in blocks(PREPARED_DVE, u, place):
                    k, q = n // 2, n % 2
                    rows = W_rows[k][:, q * HALF:(q + 1) * HALF]
                    dve.wait_ge(ld_W[k], 16)
                    dve.wait_ge(prep_full, n + 1)
                    tt(rows, fo_ps[:, q, :], rows, ALU.add).then_inc(prep_sum, 1)
                    for m in ([n - 1] if n >= 1 else []) + ([n] if n == 2 * KD - 1 else []):
                        k, q = m // 2, m % 2
                        cols = slice(q * HALF, (q + 1) * HALF)
                        dve.wait_ge(prep_hi, m + 1)
                        stt(out=w_lo[:, k, cols], in0=W_rows[k][:, cols], scalar=g_t[:, 1:2],
                            in1=w_hi[:, k, cols].bitcast(F32), op0=ALU.mult, op1=ALU.subtract).then_inc(prep_lo, 1)

            def layer_stats(b, h):
                if h == 0 and some(b):
                    dve.wait_ge(mv_done, 2 * b)
                apart(dve, dve_turns)
                for r in range(2):
                    nc.vector.bn_stats(stats[:, r, h, :], x_half(b, r, h)).then_inc(stats_done, 1)
                if h == 1:
                    if some(b):
                        dve.wait_ge(rs_step[1], RS_STEPS[1] * b)
                    dve.wait_ge(stats_done, 4 * (b + 1))
                    apart(dve, dve_turns)
                    for r in range(2):
                        nc.vector.bn_aggr(mv[:, r, :], stats[:, r, :, :]).then_inc(mv_done, 1)

            def slot(i, s):
                u = 2 * i + s
                base = TOP_STEPS * u
                if live(u, UNITS):
                    dve.wait_ge(c_evac, 2 * (u + 1))
                    apart(dve, dve_turns)
                    for t in range(TILES):
                        nc.vector.max(top[:, t, 0:8], corr[:, t, :]).then_inc(top_step, 1)
                    prepare_weights(u, "max")
                    dve.wait_ge(top_step, base + 4)
                    apart(dve, dve_turns)
                    for t in range(TILES):
                        nc.vector.match_replace(left[:, t, :], top[:, t, 0:8], corr[:, t, :], GONE
                                                ).then_inc(top_step, 1)
                    prepare_weights(u, "replaced")
                    dve.wait_ge(top_step, base + 8)
                    apart(dve, dve_turns)
                    for t in range(TILES):
                        nc.vector.max(top[:, t, 8:16], left[:, t, :]).then_inc(top_step, 1)
                    prepare_weights(u, "max again")
                    dve.wait_ge(top_step, base + 12)
                    tt(top_rel[:, :, :], top[:, :, 0:TOPK], top[:, :, 0:1].broadcast_to((P, TILES, TOPK)),
                       ALU.subtract).then_inc(top_step, 1)
                    nc.vector.memset(top[:, :, TOPK:16], GONE).then_inc(top_step, 1)
                    dve.wait_ge(top_step, base + 14)
                    apart(dve, dve_turns)
                    for t in range(TILES):
                        nc.vector.match_replace(left[:, t, :], top[:, t, 8:16], left[:, t, :], GONE
                                                ).then_inc(top_step, 1)
                    prepare_weights(u, "replaced again")
                j = u - 3
                if live(j, UNITS):
                    dve.wait_ge(ft_hi, 2 * j + 2)
                    tt(xT_lo[:, :, :].rearrange("p k n -> p (k n)"), t_ps[:, :, :].rearrange("p f n -> p (f n)"),
                       xT_hi[:, :, :].rearrange("p k n -> p (k n)").bitcast(F32), ALU.subtract).then_inc(ft_lo, 1)
                if live(u, UNITS):
                    dve.wait_ge(top_act, 2 * u + 1)
                    nc.vector.reduce_sum(top_sum[:, :], top_exp[:, :, :], mybir.AxisListType.X
                                         ).then_inc(top_step, 1)

                v = u - 1
                p2 = P2_STEPS * v
                h = 1 - s
                if live(v, UNITS):
                    def pairs(a):
                        return a.rearrange("p (g c) n -> p g c n", g=2)

                    dve.wait_ge(xw_evac, XW_FILLS * (v + 1))
                    dve.wait_ge(fix_step, FIX_STEPS * (v + 1))
                    if some(v):
                        dve.wait_ge(o_full, v)
                    else:
                        dve.wait_ge(prep_lo, 12)
                    tt(pairs(W_cross[:, :, :]), pairs(V[:, h, :, :]), pairs(Wsp[:, :, :])[:, :, ::-1, :],
                       ALU.mult).then_inc(p2_step, 1)
                if live(u, UNITS):
                    dve.wait_ge(top_act, 2 * u + 2)
                    stt(out=exp_bias[:, :], in0=log_sum[:, :], scalar=-1.0, in1=top[:, :, 0],
                        op0=ALU.mult, op1=ALU.subtract).then_inc(top_step, 1)
                if live(v, UNITS):
                    dve.wait_ge(p2_step, p2 + 1)
                    tt(Wsp[:, :, :], V[:, h, :, :], Wsp[:, :, :], ALU.mult).then_inc(p2_step, 1)
                    dve.wait_ge(p2_step, p2 + 2)
                    tt(Wsp[:, 2, :], Wsp[:, 2, :], Wsp[:, 3, :], ALU.add).then_inc(p2_step, 1)
                    stt(out=Wsp[:, 0, :], in0=Wsp[:, 1, :], scalar=mask, in1=Wsp[:, 0, :], op0=ALU.mult,
                        op1=ALU.add).then_inc(p2_step, 1)
                    tt(W_cross[:, 0::2, :], W_cross[:, 0::2, :], W_cross[:, 1::2, :], ALU.subtract
                       ).then_inc(p2_step, 1)
                if live(u, UNITS):
                    dve.wait_ge(exp_done, TILES * (u + 1))
                    stt(out=left[:, :, :], in0=left[:, :, :], scalar=0.95 * GONE, in1=prob[:, :, :],
                        op0=ALU.is_le, op1=ALU.mult).then_inc(top_step, 1)
                    dve.wait_ge(top_step, base + 21)
                    for f, op in enumerate((ALU.add, ALU.subtract)):
                        tt(prob[:, :, f * P:(f + 1) * P], left[:, :, 0:P], left[:, :, L - 1:P - 1:-1],
                           op).then_inc(top_step, 1)
                prepare_weights(u, "weights")
                if live(j, UNITS):
                    b, r = (i - 2, 1) if s == 0 else (i - 1, 0)
                    dve.wait_ge(gb_added, j + 1)
                    dve.wait_ge(f_full, j + 1)
                    tt(x_tile(b, r), x_tile(b, r), fo_ps[:, :, :].rearrange("p q n -> p (q n)"), ALU.add
                       ).then_inc(f_evac, 1)
                v = u + 1
                if live(v, UNITS):
                    p1 = P1_STEPS * v
                    K = V[:, h, 0:2, :]
                    if isinstance(u, int) and u == -1:
                        dve.wait_ge(ld_tab, 16)
                    dve.wait_ge(t_evac, T_FILLS * v + 4)
                    if some(v):
                        dve.wait_ge(c_full, 2 * v)
                    tt(Q_cross[:, :, :], Q[:, :, :], K[:, ::-1, :], ALU.mult).then_inc(p1_step, 1)
                    dve.wait_ge(p1_step, p1 + 1)
                    tt(Q[:, :, :], Q[:, :, :], K, ALU.mult).then_inc(p1_step, 1)
                    tt(Q_cross[:, 0, :], Q_cross[:, 0, :], Q_cross[:, 1, :], ALU.subtract).then_inc(p1_step, 1)
                    dve.wait_ge(p1_step, p1 + 2)
                    stt(out=Q[:, 0, :], in0=Q[:, 1, :], scalar=mask, in1=Q[:, 0, :], op0=ALU.mult, op1=ALU.add
                        ).then_inc(p1_step, 1)
                prepare_weights(u, "scores")
                if isinstance(u, int) and u == -2:
                    expert_weights()
                v = u + 1
                if live(v, UNITS):
                    if isinstance(u, int) and u == -1:
                        dve.wait_ge(inv_hi_done, 2)
                        tt(inv_lo[:, CORR:OUT], inv_corr, inv_hi[:, CORR:OUT].bitcast(F32), ALU.subtract
                           ).then_inc(inv_lo_done, 1)
                        stt(out=inv_lo[:, OUT:INVERSE], in0=inv_out, scalar=g_t[:, 0:1],
                            in1=inv_hi[:, OUT:INVERSE].bitcast(F32), op0=ALU.mult, op1=ALU.subtract
                            ).then_inc(inv_lo_done, 1)
                    dve.wait_ge(cs_hi, v + 1)
                    tt(QX_r[:, 0::2, :], QX[:, 0::2, :], QX_r[:, 1::2, :].bitcast(F32), ALU.subtract
                       ).then_inc(cs_lo, 1)
                prepare_weights(u, "end")
                v = u - 1
                if live(v, UNITS):
                    b = i - 1 if s == 0 else i
                    dve.wait_ge(o_full, v + 1)
                    rows = xr[:, b & (RING - 1), :, h * HALF:(h + 1) * HALF]
                    tt(rows, rows, fo_ps[:, :, :], ALU.add).then_inc(x1_step, 1)
                    dve.wait_ge(x1_step, v + 1)
                    layer_stats(b, h)

            all_slots(dve, slot)

        @block.gpsimd
        def _(pool):
            ptt = nc.gpsimd.tensor_tensor
            for c, value in enumerate((-0.5, EPS, -1.0, float(L), 1.0 / D, -1.0 / D, 1.0)):
                nc.gpsimd.memset(consts[:, c, :], value).then_inc(consts_ready, 1)
            pool.wait_ge(consts_ready, 7)
            one_row = consts[0:1, 6, 0:1].broadcast_to((1, HALF))
            minus_half, eps, minus_one, steps, one_dth, minus_dth = (consts[:, c, :] for c in range(6))

            def query_means(b):
                if some(b):
                    pool.wait_ge(qhat_done, 4 * b)
                pool.wait_ge(sum_done, 2 * (b + 1))
                ptt(minus_mean[:, :], row_sum[:, :], minus_dth, ALU.mult).then_inc(rs_step[0], 1)

            def query_scales(b):
                step, done = rs_step[0], RS_STEPS[0] * b
                pool.wait_ge(sq_done, 2 * (b + 1))
                ptt(var_eps[0][:, :], row_sq[:, :], one_dth, ALU.mult).then_inc(step, 1)
                pool.wait_ge(step, done + 2)
                ptt(var_eps[0][:, :], var_eps[0][:, :], eps, ALU.add).then_inc(step, 1)
                pool.wait_ge(step, done + 3)
                ptt(rstd[0][:, :], var_eps[0][:, :], minus_half, ALU.pow).then_inc(step, 1)
                pool.wait_ge(step, done + 4)
                ptt(shift[0][:, :], minus_mean[:, :], rstd[0][:, :], ALU.mult).then_inc(step, 1)

            def fold_values(w, i, s):
                if some(w):
                    pool.wait_ge(t_full, T_FILLS * w)
                pool.wait_ge(ld_v, 16 * (i + 2))
                kv = [vt[:, r, s * HALF:(s + 1) * HALF] for r in range(2)]
                ptt(ev[:, :], kv[0], kv[1], ALU.add).then_inc(kv_fold, 1)
                ptt(ov[:, :], kv[0], kv[1], ALU.subtract).then_inc(kv_fold, 1)

            def row_scales(b):
                step, done = rs_step[1], RS_STEPS[1] * b
                pool.wait_ge(mv_done, 2 * (b + 1))
                ptt(var_eps[1][:, :], mv[:, :, 1], eps, ALU.add).then_inc(step, 1)
                pool.wait_ge(step, done + 1)
                ptt(rstd[1][:, :], var_eps[1][:, :], minus_half, ALU.pow).then_inc(step, 1)
                pool.wait_ge(step, done + 2)
                ptt(shift[1][:, :], mv[:, :, 0], rstd[1][:, :], ALU.mult).then_inc(step, 1)
                pool.wait_ge(step, done + 3)
                ptt(shift[1][:, :], shift[1][:, :], minus_one, ALU.mult).then_inc(step, 1)

            def gated_bias(b, r, j):
                pool.wait_ge(xhat_done, j + 1)
                ptt(x_tile(b, r), x_tile(b, r), gbias[:, :], ALU.add).then_inc(gb_added, 1)

            def slot(i, s):
                u = 2 * i + s
                j = u - 3
                if live(j, UNITS):
                    if isinstance(j, int) and j == 0:
                        pool.wait_ge(ld_bias, 16)
                        pool.wait_ge(g_ready, 1)
                        ptt(gbias[:, :], gbias[:, :], g_t[:, 1:2].broadcast_to((P, D)), ALU.mult
                            ).then_inc(gbias_ready, 1)
                        pool.wait_ge(gbias_ready, 1)
                    b, r = (i - 2, 1) if s == 0 else (i - 1, 0)
                    gated_bias(b, r, j)
                if isinstance(u, int) and u == -2:
                    fold_values(0, i, s)
                scales = s == 0 and live(i + 1, BATCH)
                if scales:
                    query_means(i + 1)
                v = u - 1
                if live(v, UNITS):
                    for a in (1, 0):
                        pool.wait_ge(os_hi, OS_HI_STEPS * v + 3 - a)
                        ptt(WX_r[:, 4 * a:4 * a + 4:2, :], WX[:, 4 * a:4 * a + 4:2, :],
                            WX_r[:, 4 * a + 1:4 * a + 4:2, :].bitcast(F32), ALU.subtract).then_inc(os_lo, 1)
                if scales:
                    query_scales(i + 1)
                w = u + 2
                if live(w, UNITS):
                    if some(w):
                        pool.wait_ge(t_full, T_FILLS * (w - 1) + 2)
                    pool.wait_ge(qhat_done, 2 * (w + 1))
                    ptt(eq[:, :], qh[:, 0, :], qh[:, 1, :], ALU.add).then_inc(q_fold, 1)
                    ptt(oq[:, :], qh[:, 0, :], qh[:, 1, :], ALU.subtract).then_inc(q_fold, 1)
                if s == 0 and live(i - 1, BATCH):
                    if some(i - 1):
                        pool.wait_ge(xhat_done, 2 * (i - 1))
                    row_scales(i - 1)
                if live(w, UNITS) and not (isinstance(w, int) and w == 0):
                    fold_values(w, i, s)
                v = u + 1
                if live(v, UNITS):
                    h = 1 - s
                    b = i if s == 0 else i + 1
                    cols = slice(h * HALF, (h + 1) * HALF)
                    fix = FIX_STEPS * v
                    pool.wait_ge(ld_vl, 16 * (b + 1))
                    ptt(vl[0:1, cols], vl[0:1, cols], steps[0:1, 0:1].broadcast_to((1, HALF)), ALU.mult
                        ).then_inc(fix_step, 1)
                    pool.wait_ge(fix_step, fix + 1)
                    pool.wait_ge(p1_step, P1_STEPS * (v + 1))
                    ptt(V[0:1, h, 0, :], V[0:1, h, 0, :], vl[0:1, cols], ALU.add).then_inc(fix_step, 1)
                    pool.wait_ge(fix_step, fix + 2)
                    ptt(vl[:, cols], vl[:, cols], tab[:, NSIN:NSIN + 1].broadcast_to((P, HALF)), ALU.mult
                        ).then_inc(fix_step, 1)
                    pool.wait_ge(fix_step, fix + 3)
                    pool.wait_ge(t_evac, T_FILLS * (v + 1))
                    ptt(V[:, h, 3, :], V[:, h, 3, :], vl[:, cols], ALU.add).then_inc(fix_step, 1)

            all_slots(pool, slot)


def constants():
    import numpy as np
    f = np.arange(P)
    n = f + 0.5
    sine_f = f.copy()
    sine_f[0] = P
    odd = (2 * f + 1) * np.pi / L
    t = np.arange(L)
    rows = np.concatenate([t[:P], t[:P - 1:-1]])
    cos, sin = 2 * np.cos(2 * np.pi * np.outer(f, t) / L), -2 * np.sin(2 * np.pi * np.outer(f, t) / L)
    cos[0], sin[0] = 1.0, (-1.0) ** t
    scale = 1.0 / L
    forward = [
        np.cos(2 * np.pi * np.outer(n, f) / L), np.sin(2 * np.pi * np.outer(n, sine_f) / L),
        np.cos(np.outer(n, odd)), np.sin(np.outer(n, odd)),
        np.eye(P), (f > 0)[:, None], (-1.0 / np.sin(odd / 2) / np.where(f == 0, L, 1))[:, None],
    ]
    inverse = [
        cos * scale, sin * scale,
        cos[:, rows] * scale / 2, sin[:, rows] * scale / 2,
        np.cos(np.outer(odd, rows)) * scale, -np.sin(np.outer(odd, rows)) * scale,
    ]
    return [np.concatenate(t, axis=1).astype(np.float32) for t in (forward, inverse)]


def kernel(**inputs):
    import numpy as np
    import concourse.bacc as bacc
    from concourse.bass_utils import run_bass_kernel_spmd

    def paired(a):
        return np.ascontiguousarray(np.stack([a[:, :P], a[:, :P - 1:-1]], axis=2))

    data = {k: np.asarray(v) for k, v in inputs.items()}
    forward, inverse = constants()
    arrays = {
        "x": paired(data["x"]), "ctx": paired(data["ctx_4096"]),
        "v_last": np.ascontiguousarray(data["ctx_4096"][:, L - 1, :]),
        "g_xattn": data["g_xattn"], "g_ffn": data["g_ffn"], "W": data["L0_ffn_W"].T, "b": data["L0_ffn_b"],
        "A": data["L0_ffn_A"],
        "B": data["L0_ffn_B"].transpose(0, 2, 1).reshape(E * R, D), "probs": data["L0_ffn_probs"], "table": forward,
        "inverse": inverse,
    }
    arrays = {f"in_{k}": np.ascontiguousarray(v) for k, v in arrays.items()}
    nc = bacc.Bacc("TRN2", target_bir_lowering=False, num_devices=1)
    args = [nc.dram_tensor(k, v.shape, mybir.dt.from_np(v.dtype), kind="ExternalInput").ap()
            for k, v in arrays.items()]
    out = nc.dram_tensor("out", (BATCH, 2, P, D), F32, kind="ExternalOutput").ap()
    build(nc, *args, out)
    r = run_bass_kernel_spmd(nc, [arrays], core_ids=[0])
    got = r.results[0]["out"]
    return np.concatenate([got[:, 0], got[:, 1, ::-1]], axis=1)
```

```python
from contextlib import ExitStack

import concourse.bass as bass
from concourse import mybir

F32 = mybir.dt.float32
F32R = mybir.dt.float32r
BF16 = mybir.dt.bfloat16
ALU = mybir.AluOpType
ACT = mybir.ActivationFunctionType

P = 128
BATCH, L, D = 8, 256, 1024
HALF = D // 2
UNITS = 2 * BATCH
TILES = HALF // P
KD = D // P
E, R = 16, 16
TOPK = 11
GONE = -3.0e38
EPS = 1e-5

FC, FS, NC, NS, IDENT = 0, P, 2 * P, 3 * P, 4 * P
MASK, NSIN = IDENT + P, IDENT + P + 1
TABLE = NSIN + 1
EVEN, ODD = 0, 2 * L
INVERSE = ODD + 2 * L

T_FILLS = 6
XW_FILLS = 5
P1_STEPS = 4
P2_STEPS = 5
OS_HI_STEPS = 3
TOP_STEPS = 23
RS_STEPS = (5, 4)
FIX_STEPS = 4
RING = 4
PRODUCTS = {(-2, "end"): (0, 3), (-1, "scores"): (3, 5), (0, "scores"): (5, 9), (0, "end"): (9, 10),
            (1, "values"): (10, 13), (1, "outputs"): (13, 14), (2, "values"): (14, 16)}
ROUNDED = {(-2, "end"): (0, 2), (-1, "copied"): (2, 4), (0, "spectra"): (4, 5), (0, "exps"): (5, 7),
           (0, "scores"): (7, 9), (1, "logs"): (9, 11), (1, "exps"): (11, 12), (1, "copied"): (12, 14),
           (2, "exps"): (14, 15), (2, "copied"): (15, 16)}
RESTS = {(-1, "folded"): (0, 2), (-1, "end"): (2, 4), (0, "scales"): (4, 7), (0, "folded"): (7, 8), (0, "end"): (8, 9),
         (1, "means"): (9, 12), (1, "folded"): (12, 14), (2, "scales"): (14, 15), (2, "folded"): (15, 16)}


def at(v, n):
    return isinstance(v, int) and v == n


def live(v, n):
    return not isinstance(v, int) or 0 <= v < n


def some(v):
    return not isinstance(v, int) or v > 0


def most(v, n):
    return min(v, n) if isinstance(v, int) else v


def blocks(prepared, slot, place):
    return range(*prepared.get((slot, place), (0, 0))) if isinstance(slot, int) else ()


def values_first(u):
    return at(u, 0)


def next_rows(i, s):
    if isinstance(i, int) and i in (-1, 0):
        return {(-1, 0): 0, (-1, 1): 1}.get((i, s), BATCH)
    return i + 1 if s == 0 else BATCH


def apart(eng, turns):
    eng.sem_inc(turns, 1)


def build(nc, x, ctx_kv, v_last, g_attn, g_ffn, W, bias, A, B, probs, table, inverse, out):
    with ExitStack() as ctx:
        def sb(name, shape, dt=F32):
            return ctx.enter_context(nc.sbuf_tensor(name, shape, dt))

        def sem(name):
            return ctx.enter_context(nc.semaphore(name))

        def whole_and_split(name, shape):
            with nc.sbuf_tensor(name, shape, F32) as whole:
                pass
            return whole, sb(f"{name}_r", shape, F32R)

        tab = sb("tab", [P, TABLE])
        fwd_hi, fwd_lo = sb("fwd_hi", [P, IDENT], F32R), sb("fwd_lo", [P, IDENT], F32R)
        inv_hi, inv_lo = sb("inv_hi", [P, INVERSE], F32R), sb("inv_lo", [P, INVERSE], F32R)
        w_hi = sb("w_hi", [P, KD, D], F32R)
        w_lo = sb("w_lo", [P, KD, D], F32R)
        xr = sb("xr", [P, RING, 2, D])
        qh = sb("qh", [P, 2, HALF])
        vt = sb("vt", [P, 2, D])
        vl = sb("vl", [P, D])
        eq, oq = (sb(n, [P, HALF]) for n in ("eq", "oq"))
        KV, KV_r = whole_and_split("KV", [P, 4, HALF])
        ev, ov = KV[:, 0, :], KV[:, 2, :]
        QX, QX_r = whole_and_split("QX", [P, 4, HALF])
        WX, WX_r = whole_and_split("WX", [P, 8, HALF])
        Q, Q_cross = QX[:, 0:2, :], QX[:, 2:4, :]
        Wsp, W_cross = WX[:, 0:4, :], WX[:, 4:8, :]
        V = sb("V", [P, 2, 4, HALF])
        wfold = W_cross[:, 0:2, :]
        corr = sb("corr", [P, TILES, L])
        left = sb("left", [P, TILES, L])
        prob = sb("prob", [P, TILES, L])
        top = sb("top", [P, TILES, 16])
        top_rel = sb("top_rel", [P, TILES, TOPK])
        top_exp = sb("top_exp", [P, TILES, TOPK])
        top_sum, log_sum, exp_bias = (sb(n, [P, TILES]) for n in ("top_sum", "log_sum", "exp_bias"))
        xhat = sb("xhat", [P, D])
        xT_room, xT = whole_and_split("xT", [P, 2, KD, P])
        xT_hi, xT_lo = xT[:, 0, :, :], xT[:, 1, :, :]
        gbias = sb("gbias", [P, D])
        row_sum, row_sq, minus_mean = (sb(n, [P, 2]) for n in ("row_sum", "row_sq", "minus_mean"))
        stats, mv = sb("stats", [P, 2, 2, 6]), sb("mv", [P, 2, 2])
        var_eps = [sb(f"var_eps{n}", [P, 2]) for n in (1, 2)]
        rstd = [sb(f"rstd{n}", [P, 2]) for n in (1, 2)]
        shift = [sb(f"shift{n}", [P, 2]) for n in (1, 2)]
        consts = sb("consts", [P, 7, 2])
        half_g = sb("half_g", [P, 1])
        g_in, g_t = sb("g_in", [P, 2]), sb("g_t", [P, 2])
        pr = sb("pr", [P, 2])

        t_ps, xw_ps, c_ps, fo_ps = (ctx.enter_context(nc.psum_tensor(n, [P, 2, 512], F32))
                                    for n in ("t_ps", "xw_ps", "c_ps", "fo_ps"))

        pB = xr[:, 3, :, :]
        A_sb = [xhat, gbias]
        spare = [WX[:, 4:8, :].rearrange("p k n -> p (k n)"), WX[:, 0:4, :].rearrange("p k n -> p (k n)"),
                 xr[:, 2, :, :].rearrange("p r d -> p (r d)"), xT_room[:, :, :, :].rearrange("p r k n -> p (r k n)")]
        W_rows = [spare[k // 2][:, k % 2 * D:(k % 2 + 1) * D] for k in range(KD)]
        inv_room = prob[:, :, :].rearrange("p t l -> p (t l)")

        ident = tab[:, IDENT:IDENT + P]
        mask = tab[:, MASK:MASK + 1]

        ld_tab, ld_x, ld_v, ld_vl, ld_g = (sem(n) for n in ("ld_tab", "ld_x", "ld_v", "ld_vl", "ld_g"))
        ld_B, ld_A, ld_probs, ld_bias = (sem(n) for n in ("ld_B", "ld_A", "ld_probs", "ld_bias"))
        ld_W = [sem(f"ld_W{k}") for k in range(KD)]
        ld_inv, inv_hi_done, inv_lo_done = (sem(n) for n in ("ld_inv", "inv_hi_done", "inv_lo_done"))
        fwd_hi_done, fwd_lo_done, half_g_ready = (sem(n) for n in ("fwd_hi_done", "fwd_lo_done", "half_g_ready"))
        kv_hi, kv_lo = sem("kv_hi"), sem("kv_lo")
        cs_hi, cs_lo, os_hi, os_lo = (sem(n) for n in ("cs_hi", "cs_lo", "os_hi", "os_lo"))
        st_out = [sem("st_lo"), sem("st_hi")]
        g_ready, gbias_ready, consts_ready = (sem(n) for n in ("g_ready", "gbias_ready", "consts_ready"))
        pB_done, prep_full, prep_sum, prep_hi, prep_lo = (sem(n) for n in ("pB_done", "prep_full", "prep_sum",
                                                                          "prep_hi", "prep_lo"))
        xw_full, xw_evac, t_full, t_evac = (sem(n) for n in ("xw_full", "xw_evac", "t_full", "t_evac"))
        ft_full, ft_hi, ft_lo, f_full, f_evac = (sem(n) for n in ("ft_full", "ft_hi", "ft_lo", "f_full", "f_evac"))
        o_full, x1_step, c_full, c_evac = (sem(n) for n in ("o_full", "x1_step", "c_full", "c_evac"))
        top_step, top_act, exp_done = (sem(n) for n in ("top_step", "top_act", "exp_done"))
        p1_step, p2_step, nyq1, nyq2, fix_step = (sem(n) for n in ("p1_step", "p2_step", "nyq1", "nyq2", "fix_step"))
        sum_done, sq_done, stats_done, mv_done = (sem(n) for n in ("sum_done", "sq_done", "stats_done", "mv_done"))
        rs_step = [sem("rs1_step"), sem("rs2_step")]
        qhat_done, q_fold, kv_fold, xhat_done, gb_added = (sem(n) for n in ("qhat_done", "q_fold", "kv_fold",
                                                                           "xhat_done", "gb_added"))
        act_turns, dve_turns, sp_turns = (sem(n) for n in ("act_turns", "dve_turns", "sp_turns"))
        block = ctx.enter_context(nc.Block())

        def x_tile(b, r):
            return xr[:, b & (RING - 1), r, :]

        def x_half(b, r, h):
            return xr[:, b & (RING - 1), r, h * HALF:(h + 1) * HALF]

        def all_slots(eng, slot):
            for i in (-1, 0, 1):
                slot(i, 0)
                slot(i, 1)
            with eng.Fori(2, 7) as i:
                slot(i, 0)
                slot(i, 1)
            for i in (7, 8, 9):
                slot(i, 0)
                slot(i, 1)

        @block.sync
        def _(sp):
            sp.dma_start(xr[:, 0, :, :], x[0]).then_inc(ld_x, 16)
            sp.dma_start(pB, B.rearrange("(a p) o -> p a o", p=P)).then_inc(ld_B, 16)
            for q in range(2):
                sp.dma_start(A_sb[q][:, :], A.rearrange("e r d -> (e r) d")[q * P:(q + 1) * P]).then_inc(ld_A, 16)
            sp.dma_start(tab[:, :], table).then_inc(ld_tab, 16)
            for k in range(2):
                sp.dma_start(W_rows[k], W[k * P:(k + 1) * P]).then_inc(ld_W[k], 16)
            sp.dma_start(vt[:, :, :], ctx_kv[0]).then_inc(ld_v, 16)
            sp.dma_start(inv_room, inverse).then_inc(ld_inv, 16)
            sp.wait_ge(ld_x, 16)
            sp.dma_start(xr[:, 1, :, :], x[1]).then_inc(ld_x, 16)
            for k in range(2, KD):
                sp.dma_start(W_rows[k], W[k * P:(k + 1) * P]).then_inc(ld_W[k], 16)
            sp.dma_start(vl[:, :], v_last[0].partition_broadcast(P)).then_inc(ld_vl, 16)
            sp.wait_ge(kv_fold, 4)
            sp.wait_ge(ld_v, 16)
            sp.dma_start(vt[:, :, :], ctx_kv[1]).then_inc(ld_v, 16)

            def body(i):
                if at(i, 1):
                    sp.wait_ge(prep_full, 2 * KD)
                    sp.dma_start(gbias[:, :], bias.partition_broadcast(P)).then_inc(ld_bias, 16)
                if live(i - 2, BATCH):
                    sp.wait_ge(f_evac, 2 * (i - 2) + 2)
                    apart(sp, sp_turns)
                    sp.dma_start(out[i - 2, 1], x_tile(i - 2, 1)).then_inc(st_out[1], 16)
                if live(i + 1, BATCH):
                    sp.wait_ge(fix_step, FIX_STEPS * (2 * i + 2))
                    sp.wait_ge(ld_vl, 16 * (i + 1))
                    sp.dma_start(vl[:, :], v_last[i + 1].partition_broadcast(P)).then_inc(ld_vl, 16)
                if live(i + 2, BATCH):
                    if not isinstance(i, int) or i >= 2:
                        for r in range(2):
                            sp.wait_ge(st_out[r], 16 * (i - 1))
                    elif i == 0:
                        sp.wait_ge(prep_lo, 12)
                    else:
                        sp.wait_ge(prep_full, 2 * KD)
                    sp.wait_ge(ld_x, 16 * (i + 2))
                    apart(sp, sp_turns)
                    sp.dma_start(xr[:, (i + 2) & (RING - 1), :, :], x[i + 2]).then_inc(ld_x, 16)
                if live(i - 1, BATCH):
                    sp.wait_ge(f_evac, 2 * (i - 1) + 1)
                    apart(sp, sp_turns)
                    sp.dma_start(out[i - 1, 0], x_tile(i - 1, 0)).then_inc(st_out[0], 16)
                if live(i + 2, BATCH):
                    sp.wait_ge(kv_fold, 4 * (i + 2))
                    apart(sp, sp_turns)
                    sp.wait_ge(ld_v, 16 * (i + 2))
                    sp.dma_start(vt[:, :, :], ctx_kv[i + 2]).then_inc(ld_v, 16)

            body(0)
            body(1)
            with sp.Fori(2, 6) as i:
                body(i)
            for i in (6, 7, 8, 9):
                body(i)
            for r in range(2):
                sp.wait_ge(st_out[r], 16 * BATCH)

        @block.tensor
        def _(pe):
            mm = nc.tensor.matmul
            pe.wait_ge(ld_tab, 16)

            def prepare_weights(u, place):
                if at(u, 2) and place == "values":
                    pe.wait_ge(x1_step, 1)
                for n in blocks(PRODUCTS, u, place):
                    k, q = n // 2, n % 2
                    cols = slice(q * HALF, (q + 1) * HALF)
                    if n == 0:
                        pe.wait_ge(ld_A, 32)
                        pe.wait_ge(pB_done, 2)
                    if n >= 2:
                        pe.wait_ge(prep_sum, n - 1)
                    for a in range(2):
                        mm(fo_ps[:, q, :], A_sb[a][:, k * P:(k + 1) * P], pB[:, a, cols],
                           start=(a == 0), stop=False)
                    pe.wait_ge(ld_W[k], 16)
                    mm(fo_ps[:, q, :], ident, W_rows[k][:, cols], start=False, stop=True).then_inc(prep_full, 1)

            def transform(v, fills):
                for k in fills:
                    if k >= 2 or some(v):
                        pe.wait_ge(t_evac, T_FILLS * v + k - 1)
                    ps = t_ps[:, k % 2, :]
                    if k < 2:
                        c, src = ((FC, eq), (FS, oq))[k]
                        last = mm(ps, tab[:, c:c + P], src[:, :], start=True, stop=True)
                    else:
                        c, plane = ((FC, 0), (FS, 2), (NC, 2), (NS, 0))[k - 2]
                        hi, lo = KV_r[:, plane + 1, :], KV_r[:, plane, :]
                        mm(ps, fwd_hi[:, c:c + P], hi, start=True, stop=False)
                        mm(ps, fwd_lo[:, c:c + P], hi, start=False, stop=False)
                        last = mm(ps, fwd_hi[:, c:c + P], lo, start=False, stop=True)
                    last.then_inc(t_full, 1)

            def transform_values(v, fills):
                if live(v, UNITS):
                    if at(v, 0):
                        pe.wait_ge(fwd_lo_done, 1)
                    pe.wait_ge(kv_lo, v + 1)
                    transform(v, fills)

            def slot(i, s):
                u = 2 * i + s
                v = u - 1
                if live(v, UNITS):
                    pe.wait_ge(top_step, TOP_STEPS * (v + 1))
                    if some(v):
                        pe.wait_ge(xw_evac, XW_FILLS * v)
                    for f in range(2):
                        for t in range(TILES):
                            last = nc.tensor.transpose(xw_ps[:, f, t * P:(t + 1) * P],
                                                       prob[:, t, f * P:(f + 1) * P], ident)
                    last.then_inc(xw_full, 1)
                j = u - 3
                if live(u + 1, UNITS):
                    if some(j) and live(j, UNITS):
                        pe.wait_ge(ft_lo, j)
                    pe.wait_ge(q_fold, 2 * (u + 2))
                    transform(u + 1, (0, 1))
                for f in range(2):
                    if live(v, UNITS):
                        for k, (c, fold) in list(enumerate(((FC, 0), (FS, 1), (NC, 1), (NS, 0))))[2 * f:2 * f + 2]:
                            pe.wait_ge(xw_evac, XW_FILLS * v + max(k, 1))
                            mm(xw_ps[:, k % 2, :], tab[:, c:c + P], wfold[:, fold, :],
                               start=True, stop=True).then_inc(xw_full, 1)
                    if live(j, UNITS):
                        if f == 0:
                            pe.wait_ge(xhat_done, j + 1)
                            pe.wait_ge(t_evac, most(T_FILLS * (u + 1) + 2, T_FILLS * UNITS))
                            if some(j):
                                pe.wait_ge(ft_lo, j)
                        for k in range(4):
                            last = nc.tensor.transpose(t_ps[:, f, k * P:(k + 1) * P],
                                                       xhat[:, (4 * f + k) * P:(4 * f + k + 1) * P], ident)
                        last.then_inc(ft_full, 1)
                if live(j, UNITS):
                    pe.wait_ge(x1_step, most(u - 1, UNITS))
                    if some(j):
                        pe.wait_ge(f_evac, j)
                    if at(j, 0):
                        pe.wait_ge(prep_lo, 2 * KD)
                    for k in range(KD):
                        if k % 4 == 0:
                            pe.wait_ge(ft_hi, 2 * j + k // 4 + 1)
                        for wt in (w_hi, w_lo):
                            for q in range(2):
                                mm(fo_ps[:, q, :], xT_hi[:, k, :], wt[:, k, q * HALF:(q + 1) * HALF],
                                   start=(k == 0 and wt is w_hi), stop=False)
                    pe.wait_ge(ft_lo, j + 1)
                    transform_values(u + 1, (2, 3))
                    for q in range(2):
                        for k in range(KD):
                            last = mm(fo_ps[:, q, :], xT_lo[:, k, :], w_hi[:, k, q * HALF:(q + 1) * HALF],
                                      start=False, stop=(k == KD - 1))
                    last.then_inc(f_full, 1)
                prepare_weights(u, "values")
                if not live(j, UNITS):
                    transform_values(u + 1, (2, 3))
                transform_values(u + 1, (4, 5))
                prepare_weights(u, "outputs")
                v = u - 1
                if live(v, UNITS):
                    pe.wait_ge(os_hi, OS_HI_STEPS * (v + 1))
                    if some(v):
                        pe.wait_ge(x1_step, v)
                    else:
                        pe.wait_ge(inv_hi_done, 1)
                        pe.wait_ge(inv_lo_done, 1)
                    if at(v, 0):
                        pe.wait_ge(prep_sum, PRODUCTS[1, "outputs"][1])
                    if at(v, 1):
                        pe.wait_ge(prep_sum, 2 * KD)
                    if live(j, UNITS):
                        pe.wait_ge(f_evac, j + 1)
                    planes = (0, 4, 2, 6)
                    for r in range(2):
                        for k, plane in enumerate(planes):
                            c = EVEN + k * L + r * P
                            for basis in (inv_hi, inv_lo):
                                mm(fo_ps[:, r, :], basis[:, c:c + P], WX_r[:, plane + 1, :],
                                   start=(k == 0 and basis is inv_hi), stop=False)
                    pe.wait_ge(os_lo, 2 * (v + 1))
                    for r in range(2):
                        for k, plane in enumerate(planes):
                            c = EVEN + k * L + r * P
                            last = mm(fo_ps[:, r, :], inv_hi[:, c:c + P], WX_r[:, plane, :],
                                      start=False, stop=(k == 3))
                    last.then_inc(o_full, 1)
                prepare_weights(u, "scores")
                v = u + 1
                if live(v, UNITS):
                    if at(u, -1):
                        pe.wait_ge(inv_hi_done, 1)
                        pe.wait_ge(inv_lo_done, 1)
                    pe.wait_ge(cs_lo, v + 1)
                    if some(v):
                        pe.wait_ge(c_evac, 2 * v)
                    for n in range(2):
                        for t in (2 * n, 2 * n + 1):
                            ps = c_ps[:, n, (t % 2) * L:(t % 2 + 1) * L]
                            cols = slice(t * P, (t + 1) * P)
                            for part in range(2):
                                basis = slice(EVEN + part * L, EVEN + (part + 1) * L)
                                hi, lo = QX_r[:, 2 * part + 1, cols], QX_r[:, 2 * part, cols]
                                mm(ps, hi, inv_hi[:, basis], start=(part == 0), stop=False)
                                mm(ps, hi, inv_lo[:, basis], start=False, stop=False)
                                last = mm(ps, lo, inv_hi[:, basis], start=False, stop=(part == 1))
                        last.then_inc(c_full, 1)
                prepare_weights(u, "end")

            all_slots(pe, slot)

        @block.scalar
        def _(act):
            def prepare_weights(u, place):
                for n in blocks(ROUNDED, u, place):
                    k, q = n // 2, n % 2
                    cols = slice(q * HALF, (q + 1) * HALF)
                    act.wait_ge(prep_full, n + 1)
                    nc.scalar.activation(W_rows[k][:, cols], fo_ps[:, q, :], ACT.Copy, scale=g_t[:, 1:2]
                                         ).then_inc(prep_sum, 1)
                    act.wait_ge(prep_sum, n + 1)
                    nc.scalar.activation(w_hi[:, k, cols], W_rows[k][:, cols], ACT.Copy).then_inc(prep_hi, 1)

            def gates():
                act.wait_ge(ld_g, 32)
                nc.scalar.activation(g_t[:, :], g_in[:, :], ACT.Tanh).then_inc(g_ready, 1)
                act.preload_act_table_set("natural_log_exp_and_others")

            def round_table(rounded, table, loaded, done):
                act.wait_ge(loaded, 16)
                nc.scalar.activation(rounded[:, :], table, ACT.Copy).then_inc(done, 1)

            def round_values(v):
                if live(v, UNITS):
                    act.wait_ge(kv_fold, 2 * (v + 1))
                    nc.scalar.activation(KV_r[:, 1::2, :], KV[:, 0::2, :], ACT.Copy).then_inc(kv_hi, 1)

            def normalize(r, b, j):
                act.wait_ge(rs_step[1], RS_STEPS[1] * (b + 1))
                if some(j):
                    act.wait_ge(ft_full, 2 * j)
                apart(act, act_turns)
                nc.scalar.activation(xhat[:, :], x_tile(b, r), ACT.Identity, bias=shift[1][:, r:r + 1],
                                     scale=rstd[1][:, r:r + 1]).then_inc(xhat_done, 1)

            def normalize_queries(w, b, h):
                if live(w, UNITS):
                    act.wait_ge(rs_step[0], RS_STEPS[0] * (b + 1))
                    if some(w):
                        act.wait_ge(q_fold, 2 * w)
                    apart(act, act_turns)
                    for r in range(2):
                        nc.scalar.activation(qh[:, r, :], x_half(b, r, h), ACT.Identity,
                                             bias=shift[0][:, r:r + 1],
                                             scale=rstd[0][:, r:r + 1]).then_inc(qhat_done, 1)

            def copy_spectra(v, fills, h):
                for k in fills:
                    act.wait_ge(t_full, T_FILLS * v + k + 1)
                    if k == 0 and some(v):
                        act.wait_ge(c_full, 2 * v)
                    if k == 2 and some(v - 1):
                        act.wait_ge(p2_step, P2_STEPS * (v - 2) + 2)
                    dst = Q[:, k, :] if k < 2 else V[:, h, k - 2, :]
                    nc.scalar.activation(dst, t_ps[:, k % 2, :], ACT.Copy).then_inc(t_evac, 1)

            scrap = qh[:, :, :].bitcast(BF16)

            def row_sums(b):
                act.wait_ge(ld_x, 16 * (b + 1))
                if some(b):
                    act.wait_ge(q_fold, 4 * b)
                    act.wait_ge(rs_step[0], RS_STEPS[0] * b)
                apart(act, act_turns)
                for r in range(2):
                    nc.scalar.activation(scrap[:, r, :], x_tile(b, r), ACT.Identity,
                                         accum_out=row_sum[:, r:r + 1]).then_inc(sum_done, 1)

            def row_squares(b):
                act.wait_ge(rs_step[0], RS_STEPS[0] * b + 1)
                apart(act, act_turns)
                for r in range(2):
                    nc.scalar.activation(scrap[:, r, :], x_tile(b, r), ACT.Square,
                                         bias=minus_mean[:, r:r + 1],
                                         accum_out=row_sq[:, r:r + 1]).then_inc(sq_done, 1)

            def slot(i, s):
                u = 2 * i + s
                if at(u, -1):
                    round_values(0)
                    normalize_queries(1, 0, 1)
                    round_table(inv_hi, inv_room, ld_inv, inv_hi_done)
                v = u - 1
                if live(v, UNITS):
                    act.wait_ge(xw_full, XW_FILLS * v + 1)
                    if some(v):
                        act.wait_ge(o_full, v)
                    else:
                        act.wait_ge(prep_lo, 8)
                    nc.scalar.activation(wfold[:, :, :], xw_ps[:, :, :], ACT.Copy).then_inc(xw_evac, 1)
                j = u - 3
                if live(j, UNITS):
                    b, r = (i - 2, 1) if s == 0 else (i - 1, 0)
                    normalize(r, b, j)
                if live(u + 1, UNITS):
                    copy_spectra(u + 1, (0, 1), 1 - s)
                    if values_first(u):
                        copy_spectra(u + 1, (2, 3, 4, 5), 1 - s)
                prepare_weights(u, "spectra")

                def copy_weight_spectra(fills):
                    for k in fills:
                        act.wait_ge(xw_full, XW_FILLS * v + k + 2)
                        if k == 0 and at(v, 0):
                            act.wait_ge(half_g_ready, 1)
                        nc.scalar.activation(Wsp[:, k, :], xw_ps[:, k % 2, :], ACT.Copy,
                                             scale=(half_g[:, :] if k < 2 else g_t[:, 0:1])).then_inc(xw_evac, 1)

                for f in range(2):
                    if live(v, UNITS):
                        copy_weight_spectra((2 * f, 2 * f + 1))
                    if live(j, UNITS):
                        act.wait_ge(ft_full, 2 * j + f + 1)
                        nc.scalar.activation(xT_hi[:, 4 * f:4 * f + 4, :],
                                             t_ps[:, f, :].rearrange("p (k n) -> p k n", k=4),
                                             ACT.Copy).then_inc(ft_hi, 1)
                rows = next_rows(i, s)
                if not (at(u, -1) or at(u, 0)):
                    round_values(u + 1)
                if live(u, UNITS):
                    act.wait_ge(top_step, TOP_STEPS * u + 13)
                    nc.scalar.activation(top_exp[:, :, :], top_rel[:, :, :], ACT.Exp).then_inc(top_act, 1)
                    act.wait_ge(top_step, TOP_STEPS * u + 19)
                    nc.scalar.activation(log_sum[:, :], top_sum[:, :], ACT.Ln).then_inc(top_act, 1)
                prepare_weights(u, "logs")
                if at(u, 2):
                    row_sums(rows)
                if live(u, UNITS):
                    act.wait_ge(top_step, TOP_STEPS * u + 20)
                    for t in range(TILES):
                        nc.scalar.activation(prob[:, t, :], corr[:, t, :], ACT.Exp,
                                             bias=exp_bias[:, t:t + 1]).then_inc(exp_done, 1)
                prepare_weights(u, "exps")
                if live(rows, BATCH) and not (at(u, -1) or at(u, 2)):
                    row_sums(rows)
                v = u - 1
                if live(v, UNITS):
                    act.wait_ge(p2_step, P2_STEPS * v + 3)
                    nc.scalar.activation(WX_r[:, 3, :], WX[:, 2, :], ACT.Copy).then_inc(os_hi, 1)
                if live(u + 1, UNITS) and not values_first(u):
                    copy_spectra(u + 1, (2, 3), 1 - s)
                if live(v, UNITS):
                    act.wait_ge(p2_step, P2_STEPS * (v + 1))
                    nc.scalar.activation(W_cross[0:1, 0, :], Wsp[0:1, 1, :], ACT.Copy).then_inc(nyq2, 1)
                    act.wait_ge(nyq2, v + 1)
                    nc.scalar.activation(WX_r[:, 5:8:2, :], WX[:, 4:8:2, :], ACT.Copy).then_inc(os_hi, 1)
                    nc.scalar.activation(WX_r[:, 1, :], WX[:, 0, :], ACT.Copy).then_inc(os_hi, 1)
                prepare_weights(u, "values")
                if live(u + 1, UNITS) and not values_first(u):
                    copy_spectra(u + 1, (4, 5), 1 - s)
                prepare_weights(u, "copied")
                if live(rows, BATCH) and not at(u, -1):
                    row_squares(rows)
                v = u + 1
                if live(v, UNITS):
                    act.wait_ge(p1_step, P1_STEPS * v + 3)
                    nc.scalar.activation(Q_cross[0:1, 0, :], Q[0:1, 1, :], ACT.Copy).then_inc(nyq1, 1)
                    act.wait_ge(nyq1, v + 1)
                    nc.scalar.activation(QX_r[:, 3, :], QX[:, 2, :], ACT.Copy).then_inc(cs_hi, 1)
                    act.wait_ge(p1_step, P1_STEPS * (v + 1))
                    nc.scalar.activation(QX_r[:, 1, :], QX[:, 0, :], ACT.Copy).then_inc(cs_hi, 1)
                if at(u, -1):
                    round_values(1)
                    row_sums(rows)
                    row_squares(rows)
                if not at(u, -1):
                    normalize_queries(u + 2, i + 1, s)
                prepare_weights(u, "scores")
                if live(v, UNITS):
                    for n in range(2):
                        act.wait_ge(c_full, 2 * v + n + 1)
                        nc.scalar.activation(corr[:, 2 * n:2 * n + 2, :],
                                             c_ps[:, n, :].rearrange("p (t l) -> p t l", t=2),
                                             ACT.Copy).then_inc(c_evac, 1)
                if at(u, -2):
                    round_table(fwd_hi, tab[:, 0:IDENT], ld_tab, fwd_hi_done)
                prepare_weights(u, "end")

            act.dma_start(g_in[:, 0:1], g_attn.partition_broadcast(P)).then_inc(ld_g, 16)
            act.dma_start(g_in[:, 1:2], g_ffn.partition_broadcast(P)).then_inc(ld_g, 16)
            for q in range(2):
                act.dma_start(pr[:, q:q + 1],
                              probs[q * 8:(q + 1) * 8].unsqueeze(1).broadcast_to((8, R)).unsqueeze(2)
                              ).then_inc(ld_probs, 16)
            gates()
            all_slots(act, slot)

        @block.vector
        def _(dve):
            tt = nc.vector.tensor_tensor
            stt = nc.vector.scalar_tensor_tensor

            def expert_weights():
                dve.wait_ge(ld_probs, 32)
                dve.wait_ge(ld_B, 16)
                for a in range(2):
                    tt(pB[:, a, :], pB[:, a, :], pr[:, a:a + 1].broadcast_to((P, D)), ALU.mult
                       ).then_inc(pB_done, 1)

            def layer_stats(b, h):
                if h == 0 and some(b):
                    dve.wait_ge(mv_done, 2 * b)
                apart(dve, dve_turns)
                for r in range(2):
                    nc.vector.bn_stats(stats[:, r, h, :], x_half(b, r, h)).then_inc(stats_done, 1)
                if h == 1:
                    if some(b):
                        dve.wait_ge(rs_step[1], RS_STEPS[1] * b)
                    dve.wait_ge(stats_done, 4 * (b + 1))
                    apart(dve, dve_turns)
                    for r in range(2):
                        nc.vector.bn_aggr(mv[:, r, :], stats[:, r, :, :]).then_inc(mv_done, 1)

            def cross_products(v, h):
                if live(v, UNITS):
                    p1 = P1_STEPS * v
                    K = V[:, h, 0:2, :]
                    if at(v, 0):
                        dve.wait_ge(ld_tab, 16)
                    dve.wait_ge(t_evac, T_FILLS * v + 4)
                    if some(v):
                        dve.wait_ge(c_full, 2 * v)
                    tt(Q_cross[:, :, :], Q[:, :, :], K[:, ::-1, :], ALU.mult).then_inc(p1_step, 1)
                    dve.wait_ge(p1_step, p1 + 1)
                    tt(Q[:, :, :], Q[:, :, :], K, ALU.mult).then_inc(p1_step, 1)

            def cross_sums(v):
                if live(v, UNITS):
                    p1 = P1_STEPS * v
                    dve.wait_ge(p1_step, p1 + 2)
                    tt(Q_cross[:, 0, :], Q_cross[:, 0, :], Q_cross[:, 1, :], ALU.subtract).then_inc(p1_step, 1)
                    stt(out=Q[:, 0, :], in0=Q[:, 1, :], scalar=mask, in1=Q[:, 0, :], op0=ALU.mult, op1=ALU.add
                        ).then_inc(p1_step, 1)

            def slot(i, s):
                u = 2 * i + s
                base = TOP_STEPS * u
                if live(u, UNITS):
                    dve.wait_ge(c_evac, 2 * (u + 1))
                    apart(dve, dve_turns)
                    for t in range(TILES):
                        nc.vector.max(top[:, t, 0:8], corr[:, t, :]).then_inc(top_step, 1)
                    dve.wait_ge(top_step, base + 4)
                    apart(dve, dve_turns)
                    for t in range(TILES):
                        nc.vector.match_replace(left[:, t, :], top[:, t, 0:8], corr[:, t, :], GONE
                                                ).then_inc(top_step, 1)
                    dve.wait_ge(top_step, base + 8)
                    apart(dve, dve_turns)
                    for t in range(TILES):
                        nc.vector.max(top[:, t, 8:16], left[:, t, :]).then_inc(top_step, 1)
                    dve.wait_ge(top_step, base + 12)
                    tt(top_rel[:, :, :], top[:, :, 0:TOPK], top[:, :, 0:1].broadcast_to((P, TILES, TOPK)),
                       ALU.subtract).then_inc(top_step, 1)
                    nc.vector.memset(top[:, :, TOPK:16], GONE).then_inc(top_step, 1)
                    dve.wait_ge(top_step, base + 14)
                    apart(dve, dve_turns)
                    for t in range(TILES):
                        nc.vector.match_replace(left[:, t, :], top[:, t, 8:16], left[:, t, :], GONE
                                                ).then_inc(top_step, 1)
                j = u - 3
                if live(j, UNITS):
                    dve.wait_ge(ft_hi, 2 * j + 2)
                    tt(xT_lo[:, :, :].rearrange("p k n -> p (k n)"), t_ps[:, :, :].rearrange("p f n -> p (f n)"),
                       xT_hi[:, :, :].rearrange("p k n -> p (k n)").bitcast(F32), ALU.subtract).then_inc(ft_lo, 1)
                if live(u, UNITS):
                    dve.wait_ge(top_act, 2 * u + 1)
                    nc.vector.reduce_sum(top_sum[:, :], top_exp[:, :, :], mybir.AxisListType.X
                                         ).then_inc(top_step, 1)

                v = u - 1
                p2 = P2_STEPS * v
                h = 1 - s
                if live(v, UNITS):
                    def pairs(a):
                        return a.rearrange("p (g c) n -> p g c n", g=2)

                    dve.wait_ge(xw_evac, XW_FILLS * (v + 1))
                    dve.wait_ge(fix_step, FIX_STEPS * (v + 1))
                    if some(v):
                        dve.wait_ge(o_full, v)
                    else:
                        dve.wait_ge(prep_lo, 4)
                    tt(pairs(W_cross[:, :, :]), pairs(V[:, h, :, :]), pairs(Wsp[:, :, :])[:, :, ::-1, :],
                       ALU.mult).then_inc(p2_step, 1)
                if live(u, UNITS):
                    dve.wait_ge(top_act, 2 * u + 2)
                    stt(out=exp_bias[:, :], in0=log_sum[:, :], scalar=-1.0, in1=top[:, :, 0],
                        op0=ALU.mult, op1=ALU.subtract).then_inc(top_step, 1)
                if values_first(u):
                    cross_products(u + 1, 1 - s)
                    cross_sums(u + 1)
                if live(v, UNITS):
                    dve.wait_ge(p2_step, p2 + 1)
                    tt(Wsp[:, :, :], V[:, h, :, :], Wsp[:, :, :], ALU.mult).then_inc(p2_step, 1)
                    dve.wait_ge(p2_step, p2 + 2)
                    tt(Wsp[:, 2, :], Wsp[:, 2, :], Wsp[:, 3, :], ALU.add).then_inc(p2_step, 1)
                    stt(out=Wsp[:, 0, :], in0=Wsp[:, 1, :], scalar=mask, in1=Wsp[:, 0, :], op0=ALU.mult,
                        op1=ALU.add).then_inc(p2_step, 1)
                    tt(W_cross[:, 0::2, :], W_cross[:, 0::2, :], W_cross[:, 1::2, :], ALU.subtract
                       ).then_inc(p2_step, 1)
                if at(u, -1):
                    dve.wait_ge(inv_hi_done, 1)
                    tt(inv_lo[:, :], inv_room, inv_hi[:, :].bitcast(F32), ALU.subtract).then_inc(inv_lo_done, 1)
                if at(u, -2):
                    dve.wait_ge(fwd_hi_done, 1)
                    tt(fwd_lo[:, :], tab[:, 0:IDENT], fwd_hi[:, :].bitcast(F32), ALU.subtract
                       ).then_inc(fwd_lo_done, 1)
                if not values_first(u):
                    cross_products(u + 1, 1 - s)
                if live(j, UNITS):
                    b, r = (i - 2, 1) if s == 0 else (i - 1, 0)
                    dve.wait_ge(gb_added, j + 1)
                    dve.wait_ge(f_full, j + 1)
                    tt(x_tile(b, r), x_tile(b, r), fo_ps[:, :, :].rearrange("p q n -> p (q n)"), ALU.add
                       ).then_inc(f_evac, 1)
                if not values_first(u):
                    cross_sums(u + 1)
                if live(u, UNITS):
                    dve.wait_ge(exp_done, TILES * (u + 1))
                    stt(out=left[:, :, :], in0=left[:, :, :], scalar=0.95 * GONE, in1=prob[:, :, :],
                        op0=ALU.is_le, op1=ALU.mult).then_inc(top_step, 1)
                    dve.wait_ge(top_step, base + 21)
                    for f, op in enumerate((ALU.add, ALU.subtract)):
                        tt(prob[:, :, f * P:(f + 1) * P], left[:, :, 0:P], left[:, :, P:L],
                           op).then_inc(top_step, 1)
                v = u + 1
                if live(v, UNITS):
                    dve.wait_ge(cs_hi, 2 * (v + 1))
                    tt(QX_r[:, 0::2, :], QX[:, 0::2, :], QX_r[:, 1::2, :].bitcast(F32), ALU.subtract
                       ).then_inc(cs_lo, 1)
                v = u - 1
                if live(v, UNITS):
                    b = i - 1 if s == 0 else i
                    dve.wait_ge(o_full, v + 1)
                    rows = xr[:, b & (RING - 1), :, h * HALF:(h + 1) * HALF]
                    tt(rows, rows, fo_ps[:, :, :], ALU.add).then_inc(x1_step, 1)
                    dve.wait_ge(x1_step, v + 1)
                    layer_stats(b, h)

            expert_weights()
            all_slots(dve, slot)

        @block.gpsimd
        def _(pool):
            ptt = nc.gpsimd.tensor_tensor
            for c, value in enumerate((-0.5, EPS, -1.0, float(L), 1.0 / D, -1.0 / D, 0.5)):
                nc.gpsimd.memset(consts[:, c, :], value).then_inc(consts_ready, 1)
            pool.wait_ge(consts_ready, 7)
            half = consts[:, 6, 0:1]
            minus_half, eps, minus_one, steps, one_dth, minus_dth = (consts[:, c, :] for c in range(6))

            def query_means(b):
                if some(b):
                    pool.wait_ge(qhat_done, 4 * b)
                pool.wait_ge(sum_done, 2 * (b + 1))
                ptt(minus_mean[:, :], row_sum[:, :], minus_dth, ALU.mult).then_inc(rs_step[0], 1)

            def query_scales(b):
                step, done = rs_step[0], RS_STEPS[0] * b
                pool.wait_ge(sq_done, 2 * (b + 1))
                ptt(var_eps[0][:, :], row_sq[:, :], one_dth, ALU.mult).then_inc(step, 1)
                pool.wait_ge(step, done + 2)
                ptt(var_eps[0][:, :], var_eps[0][:, :], eps, ALU.add).then_inc(step, 1)
                pool.wait_ge(step, done + 3)
                ptt(rstd[0][:, :], var_eps[0][:, :], minus_half, ALU.pow).then_inc(step, 1)
                pool.wait_ge(step, done + 4)
                ptt(shift[0][:, :], minus_mean[:, :], rstd[0][:, :], ALU.mult).then_inc(step, 1)

            def rest_of_values(v):
                if live(v, UNITS):
                    pool.wait_ge(kv_hi, v + 1)
                    ptt(KV_r[:, 0::2, :], KV[:, 0::2, :], KV_r[:, 1::2, :].bitcast(F32), ALU.subtract
                        ).then_inc(kv_lo, 1)

            def fold_values(w, i, s):
                if some(w):
                    pool.wait_ge(t_full, T_FILLS * w)
                pool.wait_ge(ld_v, 16 * (i + 2))
                kv = [vt[:, r, s * HALF:(s + 1) * HALF] for r in range(2)]
                ptt(ev, kv[0], kv[1], ALU.add).then_inc(kv_fold, 1)
                ptt(ov, kv[0], kv[1], ALU.subtract).then_inc(kv_fold, 1)

            def row_scales(b):
                step, done = rs_step[1], RS_STEPS[1] * b
                pool.wait_ge(mv_done, 2 * (b + 1))
                ptt(var_eps[1][:, :], mv[:, :, 1], eps, ALU.add).then_inc(step, 1)
                pool.wait_ge(step, done + 1)
                ptt(rstd[1][:, :], var_eps[1][:, :], minus_half, ALU.pow).then_inc(step, 1)
                pool.wait_ge(step, done + 2)
                ptt(shift[1][:, :], mv[:, :, 0], rstd[1][:, :], ALU.mult).then_inc(step, 1)
                pool.wait_ge(step, done + 3)
                ptt(shift[1][:, :], shift[1][:, :], minus_one, ALU.mult).then_inc(step, 1)

            def gated_bias(b, r, j):
                pool.wait_ge(xhat_done, j + 1)
                ptt(x_tile(b, r), x_tile(b, r), gbias[:, :], ALU.add).then_inc(gb_added, 1)

            def prepare_weights(u, place):
                for n in blocks(RESTS, u, place):
                    k, q = n // 2, n % 2
                    cols = slice(q * HALF, (q + 1) * HALF)
                    pool.wait_ge(prep_hi, n + 1)
                    ptt(w_lo[:, k, cols], W_rows[k][:, cols], w_hi[:, k, cols].bitcast(F32), ALU.subtract
                        ).then_inc(prep_lo, 1)

            def slot(i, s):
                u = 2 * i + s
                j = u - 3
                if live(j, UNITS):
                    b, r = (i - 2, 1) if s == 0 else (i - 1, 0)
                    gated_bias(b, r, j)
                rows = next_rows(i, s)
                if not at(u, 0):
                    rest_of_values(u + 1)
                if at(u, -1):
                    pool.wait_ge(g_ready, 1)
                    ptt(half_g[:, :], g_t[:, 0:1], half, ALU.mult).then_inc(half_g_ready, 1)
                if live(rows, BATCH) and not at(u, -1):
                    query_means(rows)
                if at(u, 2):
                    pool.wait_ge(ld_bias, 16)
                    pool.wait_ge(g_ready, 1)
                    ptt(gbias[:, :], gbias[:, :], g_t[:, 1:2].broadcast_to((P, D)), ALU.mult).then_inc(gbias_ready, 1)
                    pool.wait_ge(gbias_ready, 1)
                prepare_weights(u, "means")
                v = u - 1
                if live(v, UNITS):
                    for a in (1, 0):
                        pool.wait_ge(os_hi, OS_HI_STEPS * v + 3 - a)
                        ptt(WX_r[:, 4 * a:4 * a + 4:2, :], WX[:, 4 * a:4 * a + 4:2, :],
                            WX_r[:, 4 * a + 1:4 * a + 4:2, :].bitcast(F32), ALU.subtract).then_inc(os_lo, 1)
                prepare_weights(u, "scales")
                if live(rows, BATCH) and not at(u, -1):
                    query_scales(rows)
                w = u + 2
                if live(w, UNITS):
                    if some(w):
                        pool.wait_ge(t_full, T_FILLS * (w - 1) + 2)
                    pool.wait_ge(qhat_done, 2 * (w + 1))
                    ptt(eq[:, :], qh[:, 0, :], qh[:, 1, :], ALU.add).then_inc(q_fold, 1)
                    ptt(oq[:, :], qh[:, 0, :], qh[:, 1, :], ALU.subtract).then_inc(q_fold, 1)
                prepare_weights(u, "folded")
                if s == 0 and live(i - 1, BATCH):
                    if some(i - 1):
                        pool.wait_ge(xhat_done, 2 * (i - 1))
                    row_scales(i - 1)
                if live(w, UNITS):
                    fold_values(w, i, s)
                if at(u, -1):
                    rest_of_values(1)
                    query_means(1)
                    query_scales(1)
                v = u + 1
                if live(v, UNITS):
                    h = 1 - s
                    b = i if s == 0 else i + 1
                    cols = slice(h * HALF, (h + 1) * HALF)
                    fix = FIX_STEPS * v
                    pool.wait_ge(ld_vl, 16 * (b + 1))
                    ptt(vl[0:1, cols], vl[0:1, cols], steps[0:1, 0:1].broadcast_to((1, HALF)), ALU.mult
                        ).then_inc(fix_step, 1)
                    pool.wait_ge(fix_step, fix + 1)
                    pool.wait_ge(p1_step, P1_STEPS * (v + 1))
                    ptt(V[0:1, h, 0, :], V[0:1, h, 0, :], vl[0:1, cols], ALU.add).then_inc(fix_step, 1)
                    pool.wait_ge(fix_step, fix + 2)
                    ptt(vl[:, cols], vl[:, cols], tab[:, NSIN:NSIN + 1].broadcast_to((P, HALF)), ALU.mult
                        ).then_inc(fix_step, 1)
                    pool.wait_ge(fix_step, fix + 3)
                    pool.wait_ge(t_evac, T_FILLS * (v + 1))
                    ptt(V[:, h, 3, :], V[:, h, 3, :], vl[:, cols], ALU.add).then_inc(fix_step, 1)

                prepare_weights(u, "end")

            all_slots(pool, slot)


def constants():
    import numpy as np
    f = np.arange(P)
    n = f + 0.5
    sine_f = f.copy()
    sine_f[0] = P
    odd = (2 * f + 1) * np.pi / L
    t = np.arange(L)
    rows = np.concatenate([t[:P], t[:P - 1:-1]])
    cos, sin = 2 * np.cos(2 * np.pi * np.outer(f, t) / L), -2 * np.sin(2 * np.pi * np.outer(f, t) / L)
    cos[0], sin[0] = 1.0, (-1.0) ** t
    scale = 1.0 / L
    forward = [
        np.cos(2 * np.pi * np.outer(n, f) / L), np.sin(2 * np.pi * np.outer(n, sine_f) / L),
        np.cos(np.outer(n, odd)), np.sin(np.outer(n, odd)),
        np.eye(P), (f > 0)[:, None], (-1.0 / np.sin(odd / 2) / np.where(f == 0, L, 1))[:, None],
    ]
    inverse = [
        cos[:, rows] * scale, sin[:, rows] * scale,
        np.cos(np.outer(odd, rows)) * scale, -np.sin(np.outer(odd, rows)) * scale,
    ]
    return [np.concatenate(t, axis=1).astype(np.float32) for t in (forward, inverse)]


def kernel(**inputs):
    import numpy as np
    import concourse.bacc as bacc
    from concourse.bass_utils import run_bass_kernel_spmd

    def paired(a):
        return np.ascontiguousarray(np.stack([a[:, :P], a[:, :P - 1:-1]], axis=2))

    data = {k: np.asarray(v) for k, v in inputs.items()}
    forward, inverse = constants()
    arrays = {
        "x": paired(data["x"]), "ctx": paired(data["ctx_4096"]),
        "v_last": np.ascontiguousarray(data["ctx_4096"][:, L - 1, :]),
        "g_xattn": data["g_xattn"], "g_ffn": data["g_ffn"], "W": data["L0_ffn_W"].T, "b": data["L0_ffn_b"],
        "A": data["L0_ffn_A"],
        "B": data["L0_ffn_B"].transpose(0, 2, 1).reshape(E * R, D), "probs": data["L0_ffn_probs"], "table": forward,
        "inverse": inverse,
    }
    arrays = {f"in_{k}": np.ascontiguousarray(v) for k, v in arrays.items()}
    nc = bacc.Bacc("TRN2", target_bir_lowering=False, num_devices=1)
    args = [nc.dram_tensor(k, v.shape, mybir.dt.from_np(v.dtype), kind="ExternalInput").ap()
            for k, v in arrays.items()]
    out = nc.dram_tensor("out", (BATCH, 2, P, D), F32, kind="ExternalOutput").ap()
    build(nc, *args, out)
    r = run_bass_kernel_spmd(nc, [arrays], core_ids=[0])
    got = r.results[0]["out"]
    return np.concatenate([got[:, 0], got[:, 1, ::-1]], axis=1)
```
